# Optimizing a Trainium2 kernel written in Bass

```python
import numpy as np
import jax
import jax.numpy as jnp

def _softmax(x, axis=-1):
    return jax.nn.softmax(x, axis=axis)

def _gelu(x):
    return jax.nn.gelu(x, approximate=True)

def _silu(x):
    return jax.nn.silu(x)

def _sigmoid(x):
    return jax.nn.sigmoid(x)

def _layernorm(x, axis=-1, eps=1e-05):
    m = jnp.mean(x, axis=axis, keepdims=True)
    v = jnp.var(x, axis=axis, keepdims=True)
    return (x - m) / jnp.sqrt(v + eps)

def _scatter_add(tgt, idx, src, axis=0):
    return tgt.at[idx].add(src)

def _segment_sum(src, seg, n):
    return jax.ops.segment_sum(src, seg, n)
kernel_name = 'mk_prb_d1_jaxref_r4_770b30'

def setup_inputs(seed: int=0):
    np.random.seed(seed)
    _w = jnp.asarray

    def _L0_attn_setup():
        import jax, jax.numpy as jnp
        import numpy as np
        import math
        B, T, C, NH = (4, 512, 256, 16)
        HS = C // NH

        def rope_cache(dim, max_pos):
            half = dim // 2
            inv_freq = 1.0 / 10000.0 ** (jnp.arange(half, dtype=jnp.float32) * 2.0 / dim)
            ang = jnp.arange(max_pos, dtype=jnp.float32)[:, None] * inv_freq[None, :]
            return (jnp.cos(ang), jnp.sin(ang))

        def apply_rope(x, cos, sin):
            x0 = x[..., 0::2]
            x1 = x[..., 1::2]
            c = cos[None, None, :, :]
            s = sin[None, None, :, :]
            r0 = x0 * c - x1 * s
            r1 = x0 * s + x1 * c
            return jnp.stack([r0, r1], axis=-1).reshape(x.shape)
        key = jax.random.key(seed)
        ks = jax.random.split(key, 5)
        sc = 1.0 / math.sqrt(C)
        return {'x': jax.random.normal(ks[0], (B, T, C), jnp.float32), 'Wq': jax.random.normal(ks[1], (C, C), jnp.float32) * sc, 'bq': jnp.zeros((C,), jnp.float32), 'Wk': jax.random.normal(ks[2], (C, C), jnp.float32) * sc, 'bk': jnp.zeros((C,), jnp.float32), 'Wv': jax.random.normal(ks[3], (C, C), jnp.float32) * sc, 'bv': jnp.zeros((C,), jnp.float32), 'Wp': jax.random.normal(ks[4], (C, C), jnp.float32) * sc, 'bp': jnp.zeros((C,), jnp.float32)}
    _L0_attn_in = _L0_attn_setup()

    def _L0_ffn_setup():
        import jax, jax.numpy as jnp
        import numpy as np
        B, S, DIM = (4, 1024, 256)
        BASE_COUPLING = 0.1
        NUM_CYCLES = 3

        def _gelu(x):
            return jax.nn.gelu(x, approximate=False)

        def _coupling_net(h, w1, b1, w2, b2, w3, b3, w4, b4):
            h = _gelu(h @ w1 + b1)
            h = _gelu(h @ w2 + b2)
            h = _gelu(h @ w3 + b3)
            return jax.nn.sigmoid(h @ w4 + b4)

        def _global_net(h, w1, b1, w2, b2, w3, b3):
            h = _gelu(h @ w1 + b1)
            h = _gelu(h @ w2 + b2)
            return jax.nn.sigmoid(h @ w3 + b3)

        def _twist(x):
            o_r, o_i, p_r, p_i = jnp.split(x, 4, axis=-1)
            return jnp.concatenate([p_r, -p_i, -o_r, o_i], axis=-1)
        key = jax.random.key(seed)
        ks = jax.random.split(key, 9)
        d = DIM

        def w(k, fan_in, fan_out):
            return jax.random.normal(k, (fan_in, fan_out), dtype=jnp.float32) / np.sqrt(fan_in).astype(np.float32)
        inp = {'x': jax.random.normal(ks[0], (B, S, d), dtype=jnp.float32)}
        cn_dims = [(d, d), (d, d // 2), (d // 2, d // 4), (d // 4, 1)]
        for i, (a, b) in enumerate(cn_dims):
            inp[f'cn_w{i + 1}'] = w(ks[1 + i], a, b)
            inp[f'cn_b{i + 1}'] = jnp.zeros((b,), dtype=jnp.float32)
        gc_dims = [(d, d // 2), (d // 2, d // 4), (d // 4, 1)]
        for i, (a, b) in enumerate(gc_dims):
            inp[f'gc_w{i + 1}'] = w(ks[5 + i], a, b)
            inp[f'gc_b{i + 1}'] = jnp.zeros((b,), dtype=jnp.float32)
        inp['adaptive_range'] = jnp.full((1,), 0.2, dtype=jnp.float32)
        return inp
    _L0_ffn_in = _L0_ffn_setup()
    _d = {'L0_attn_x': _L0_attn_in['x'], 'L0_attn_Wq': _L0_attn_in['Wq'], 'L0_attn_bq': _L0_attn_in['bq'], 'L0_attn_Wk': _L0_attn_in['Wk'], 'L0_attn_bk': _L0_attn_in['bk'], 'L0_attn_Wv': _L0_attn_in['Wv'], 'L0_attn_bv': _L0_attn_in['bv'], 'L0_attn_Wp': _L0_attn_in['Wp'], 'L0_attn_bp': _L0_attn_in['bp'], 'L0_ffn_cn_w1': _L0_ffn_in['cn_w1'], 'L0_ffn_cn_b1': _L0_ffn_in['cn_b1'], 'L0_ffn_cn_w2': _L0_ffn_in['cn_w2'], 'L0_ffn_cn_b2': _L0_ffn_in['cn_b2'], 'L0_ffn_cn_w3': _L0_ffn_in['cn_w3'], 'L0_ffn_cn_b3': _L0_ffn_in['cn_b3'], 'L0_ffn_cn_w4': _L0_ffn_in['cn_w4'], 'L0_ffn_cn_b4': _L0_ffn_in['cn_b4'], 'L0_ffn_gc_w1': _L0_ffn_in['gc_w1'], 'L0_ffn_gc_b1': _L0_ffn_in['gc_b1'], 'L0_ffn_gc_w2': _L0_ffn_in['gc_w2'], 'L0_ffn_gc_b2': _L0_ffn_in['gc_b2'], 'L0_ffn_gc_w3': _L0_ffn_in['gc_w3'], 'L0_ffn_gc_b3': _L0_ffn_in['gc_b3'], 'L0_ffn_adaptive_range': _L0_ffn_in['adaptive_range']}
    _x0 = _d['L0_attn_x']
    _d['L0_attn_x'] = jax.random.normal(jax.random.fold_in(jax.random.key(seed), 1), (2, 2048, 256), dtype=_x0.dtype)
    del _x0
    return _d

def reference(L0_attn_x, L0_attn_Wq, L0_attn_bq, L0_attn_Wk, L0_attn_bk, L0_attn_Wv, L0_attn_bv, L0_attn_Wp, L0_attn_bp, L0_ffn_cn_w1, L0_ffn_cn_b1, L0_ffn_cn_w2, L0_ffn_cn_b2, L0_ffn_cn_w3, L0_ffn_cn_b3, L0_ffn_cn_w4, L0_ffn_cn_b4, L0_ffn_gc_w1, L0_ffn_gc_b1, L0_ffn_gc_w2, L0_ffn_gc_b2, L0_ffn_gc_w3, L0_ffn_gc_b3, L0_ffn_adaptive_range):

    def _L0_attn_ref(x, Wq, bq, Wk, bk, Wv, bv, Wp, bp):
        import jax, jax.numpy as jnp
        import numpy as np
        import math
        B, T, C, NH = (4, 512, 256, 16)
        HS = C // NH

        def rope_cache(dim, max_pos):
            half = dim // 2
            inv_freq = 1.0 / 10000.0 ** (jnp.arange(half, dtype=jnp.float32) * 2.0 / dim)
            ang = jnp.arange(max_pos, dtype=jnp.float32)[:, None] * inv_freq[None, :]
            return (jnp.cos(ang), jnp.sin(ang))

        def apply_rope(x, cos, sin):
            x0 = x[..., 0::2]
            x1 = x[..., 1::2]
            c = cos[None, None, :, :]
            s = sin[None, None, :, :]
            r0 = x0 * c - x1 * s
            r1 = x0 * s + x1 * c
            return jnp.stack([r0, r1], axis=-1).reshape(x.shape)
        Bx, Tx, Cx = x.shape

        def split_heads(y):
            return y.reshape(Bx, Tx, NH, HS).transpose(0, 2, 1, 3)
        q = split_heads(x @ Wq + bq)
        k = split_heads(x @ Wk + bk)
        v = split_heads(x @ Wv + bv)
        cos, sin = rope_cache(HS, Tx)
        q = apply_rope(q, cos, sin)
        k = apply_rope(k, cos, sin)
        att = jnp.einsum('bhqd,bhkd->bhqk', q, k) * (1.0 / math.sqrt(HS))
        causal = jnp.tril(jnp.ones((Tx, Tx), bool))
        att = jnp.where(causal[None, None, :, :], att, jnp.float32(-10000000000.0))
        att = jax.nn.softmax(att, axis=-1)
        y = jnp.einsum('bhqk,bhkd->bhqd', att, v)
        y = y.transpose(0, 2, 1, 3).reshape(Bx, Tx, Cx)
        return y @ Wp + bp

    def _L0_ffn_ref(x, cn_w1, cn_b1, cn_w2, cn_b2, cn_w3, cn_b3, cn_w4, cn_b4, gc_w1, gc_b1, gc_w2, gc_b2, gc_w3, gc_b3, adaptive_range):
        import jax, jax.numpy as jnp
        import numpy as np
        B, S, DIM = (4, 1024, 256)
        BASE_COUPLING = 0.1
        NUM_CYCLES = 3

        def _gelu(x):
            return jax.nn.gelu(x, approximate=False)

        def _coupling_net(h, w1, b1, w2, b2, w3, b3, w4, b4):
            h = _gelu(h @ w1 + b1)
            h = _gelu(h @ w2 + b2)
            h = _gelu(h @ w3 + b3)
            return jax.nn.sigmoid(h @ w4 + b4)

        def _global_net(h, w1, b1, w2, b2, w3, b3):
            h = _gelu(h @ w1 + b1)
            h = _gelu(h @ w2 + b2)
            return jax.nn.sigmoid(h @ w3 + b3)

        def _twist(x):
            o_r, o_i, p_r, p_i = jnp.split(x, 4, axis=-1)
            return jnp.concatenate([p_r, -p_i, -o_r, o_i], axis=-1)
        global_context = x.mean(axis=1, keepdims=True)
        gf = _global_net(global_context, gc_w1, gc_b1, gc_w2, gc_b2, gc_w3, gc_b3)
        out = x
        for _ in range(NUM_CYCLES):
            tf = _coupling_net(out, cn_w1, cn_b1, cn_w2, cn_b2, cn_w3, cn_b3, cn_w4, cn_b4)
            combined = 0.7 * gf + 0.3 * tf
            coupling = BASE_COUPLING + adaptive_range * (combined - 0.5) * 2.0
            out = out + coupling * _twist(out)
        return out
    x = L0_attn_x
    xn = _layernorm(x, axis=-1)
    x = x + _L0_attn_ref(xn, L0_attn_Wq, L0_attn_bq, L0_attn_Wk, L0_attn_bk, L0_attn_Wv, L0_attn_bv, L0_attn_Wp, L0_attn_bp) + _L0_ffn_ref(xn, L0_ffn_cn_w1, L0_ffn_cn_b1, L0_ffn_cn_w2, L0_ffn_cn_b2, L0_ffn_cn_w3, L0_ffn_cn_b3, L0_ffn_cn_w4, L0_ffn_cn_b4, L0_ffn_gc_w1, L0_ffn_gc_b1, L0_ffn_gc_w2, L0_ffn_gc_b2, L0_ffn_gc_w3, L0_ffn_gc_b3, L0_ffn_adaptive_range)
    return x

_drawn_inputs = setup_inputs


def setup_inputs(seed=0):
    import zlib

    import numpy as np

    out = dict(_drawn_inputs(seed))
    spreads = {'L0_attn_bq': (0.0, 0.8),
     'L0_attn_bk': (0.0, 0.8),
     'L0_attn_bv': (0.0, 0.1),
     'L0_attn_bp': (0.0, 0.1),
     'L0_ffn_cn_b1': (0.0, 2.0),
     'L0_ffn_cn_b2': (0.0, 2.0),
     'L0_ffn_cn_b3': (0.0, 2.0),
     'L0_ffn_gc_b1': (0.0, 0.8),
     'L0_ffn_gc_b2': (0.0, 0.8)}
    factors = {'L0_ffn_cn_w1': 7.436,
     'L0_ffn_cn_w2': 7.791,
     'L0_ffn_cn_w3': 6.24,
     'L0_ffn_cn_w4': 6.973,
     'L0_ffn_gc_w1': 8.0,
     'L0_ffn_gc_w2': 8.0,
     'L0_ffn_gc_w3': 5.699}
    for name, (base, spread) in spreads.items():
        noise = np.random.default_rng([zlib.crc32(name.encode()), seed]).standard_normal(out[name].shape)
        drawn = base * np.exp(spread * noise) if base else spread * noise
        out[name] = jnp.asarray(drawn.astype(out[name].dtype))
    for name, factor in factors.items():
        out[name] = (out[name] * factor).astype(out[name].dtype)
    return out
```

```python
from contextlib import ExitStack

import numpy as np

import concourse.bass as bass
from concourse import mybir

ALU = mybir.AluOpType
ACT = mybir.ActivationFunctionType
AX_X = mybir.AxisListType.X
F32 = mybir.dt.float32
BF16 = mybir.dt.bfloat16

P = 128
B, T, C, NH = 2, 2048, 256, 16
HS = C // NH
CT = C // P
NI = B * CT
GH = 4
GROUPS = 2
TILES = T // P
QB = 512
CHUNKS = T // QB
TPC = QB // P
QKV = 3 * P
SPLITS = 3
SLOTS = [(0, 0), (1, 0), (2, 0), (0, 1), (1, 1), (0, 2)]
ROWS = HS * len(SLOTS)
SHIFT = ROWS
KROWS = ROWS + SPLITS
VW = HS + 1
SCALE = float(HS) ** -0.5
NEG = -1.0e30
EPS = 1e-5
H3 = 64
CYCLES = 3
PAIRS = B * T // (2 * QB)
LEAD = 72

STEPS = [(c, kt, max(0, kt * P - c * QB)) for c in range(CHUNKS) for kt in range(TPC * (c + 1))]
STRIPS = [(t, kb, min(QB, P * (t + 1) - QB * kb)) for t in range(TILES) for kb in range(t // TPC + 1)]
NS = len(STEPS)
BODY = GROUPS * NS
BLOCKS = sum(w for _, _, w in STRIPS) // P


def strips_before(work):
    n, done = 0, 0
    while done < work:
        done += STRIPS[n % len(STRIPS)][2] // P
        n += 1
    return n


def step_work(n):
    return sum(QB - lo for _, _, lo in STEPS[:n]) // P


def strips_at(s):
    g, n = divmod(s, NS)
    a = strips_before(step_work(n) + LEAD) if n else strips_before(LEAD)
    b = strips_before(step_work(n + 1) + LEAD)
    return [(g + k // len(STRIPS), k % len(STRIPS)) for k in range(a, b)]


EARLY_STRIPS = [(0, k) for k in range(strips_before(LEAD))]


def last_of_chunk(k):
    t = STRIPS[k][0]
    last = k + 1 == len(STRIPS) or STRIPS[k + 1][0] != t
    return t // TPC if last and t % TPC == TPC - 1 else None


def round_jobs(last):
    at = [[] for _ in range(BODY + 1)]
    for s in range(BODY):
        for g, k in strips_at(s):
            c = last_of_chunk(k)
            if c is not None and not (last and g == GROUPS):
                at[min(s + 1, BODY)].append(("shift", g, c))
    n = 0
    for s in range(BODY):
        if ends_block(s):
            at[min(s + 2, BODY)].append(("out", n))
            n += 1
    if not last:
        s = 8
        for job in project_order():
            while at[s]:
                s += 1
            at[s].append(job)
            s += 1
    return at


def project_order():
    jobs = [("proj", 0)]
    for t in range(1, TILES):
        jobs += [("proj", t), ("turn", t - 1)]
    return jobs + [("turn", TILES - 1)]


RING = 3


def ring_distance(n):
    return RING if n >= A_ROUND % RING else A_ROUND % RING


def ends_block(s):
    c, kt, _ = STEPS[s % NS]
    return kt == TPC * (c + 1) - 1


def diagonal(s):
    c, kt, _ = STEPS[s % NS]
    return kt >= TPC * c


DIAG = [sum(diagonal(x) for x in range(s)) for s in range(BODY + 1)]
ENDS = [sum(ends_block(x) for x in range(s)) for s in range(BODY + 1)]
UNITS = [GH * sum(len(strips_at(x)) for x in range(s)) for s in range(BODY + 1)]
EARLY_UNITS = GH * len(EARLY_STRIPS)
A_ROUND = BODY * GH
assert A_ROUND == UNITS[BODY] and A_ROUND % RING > 0
EARLY_JOBS = len(project_order()) + sum(last_of_chunk(k) is not None for _, k in EARLY_STRIPS)
LOOP_JOBS, LAST_JOBS = round_jobs(False), round_jobs(True)
JOBS_A_ROUND = sum(map(len, LOOP_JOBS))
STACK_DMAS = len(SLOTS) * 2
SHIFT_DMAS = SPLITS * GH


def build(nc, x, wqkv, bqkv, wp, bp, cos, sin, ident_in, ffn, out, y_dram):
    x_tiles = x.rearrange("b (t p) c -> p (b t) c", p=P)
    out_tiles = out.rearrange("b (t p) c -> p (b t) c", p=P)
    NT = B * TILES
    with ExitStack() as ctx:
        def sem(name):
            return ctx.enter_context(nc.semaphore(name))

        def sb(scope, name, shape, dt=F32):
            return scope.enter_context(nc.sbuf_tensor(name, shape, dt))

        def pb(scope, name, shape):
            return scope.enter_context(nc.psum_tensor(name, shape, F32))

        xnT = sb(ctx, "xnT", [P, CT, B * T])
        ident = sb(ctx, "ident", [P, P])
        wp_sb = sb(ctx, "wp_sb", [P, CT, C])
        bp_sb = sb(ctx, "bp_sb", [P, CT])
        w1 = sb(ctx, "w1", [P, CT, C])
        b1 = sb(ctx, "b1", [P, CT])
        w2 = sb(ctx, "w2", [P, CT, P])
        b2 = sb(ctx, "b2", [P, 1])
        w3 = sb(ctx, "w3", [P, H3])
        b3 = sb(ctx, "b3", [P, 1])
        w4 = sb(ctx, "w4", [P, 1])
        w4_wide = sb(ctx, "w4_wide", [P, 2, P])
        b4 = sb(ctx, "b4", [P, 1])
        gw1 = sb(ctx, "gw1", [P, CT, P])
        gb1 = sb(ctx, "gb1", [P, 1])
        gw2 = sb(ctx, "gw2", [P, H3])
        gb2 = sb(ctx, "gb2", [H3, 1])
        gw3 = sb(ctx, "gw3", [H3, 1])
        gw3_wide = sb(ctx, "gw3_wide", [H3, P])
        gb3 = sb(ctx, "gb3", [P, 1])
        ar = sb(ctx, "ar", [P, 1])
        sign = sb(ctx, "sign", [P, 1])
        swing = sb(ctx, "swing", [P, 1])
        base = sb(ctx, "base", [P, B])
        xsum = sb(ctx, "xsum", [P, CT, B])
        gh1 = sb(ctx, "gh1", [P, B])
        gh2 = sb(ctx, "gh2", [H3, B])
        gtanh = sb(ctx, "gtanh", [P, B])

        with ExitStack() as s1:
            x_in = sb(s1, "x_in", [P, NT, C])
            stats = sb(s1, "stats", [P, NT, 6])
            meanvar = sb(s1, "meanvar", [P, NT, 2])
            std = sb(s1, "std", [P, NT])
            rstd = sb(s1, "rstd", [P, NT])
            ps_x = pb(s1, "ps_x", [P, 2, CT, QB])

        with ExitStack() as s2:
            qst = [sb(s2, f"qst{g}", [P, GH, T], BF16) for g in range(GROUPS)]
            kst = [sb(s2, f"kst{g}", [P, GH, T], BF16) for g in range(GROUPS)]
            parts = sb(s2, "parts", [P, 2, SPLITS, T], BF16)
            probs = sb(s2, "probs", [P, 2, GH, QB])
            vcur = [sb(s2, f"vcur{g}", [P, TILES, GH, VW]) for g in range(GROUPS)]
            vnext = sb(s2, "vnext", [P, GROUPS, TILES, GH, VW])
            xwin = sb(s2, "xwin", [P, 2, CT, QB])
            wcur = sb(s2, "wcur", [P, CT, QKV])
            bcur = sb(s2, "bcur", [P, QKV])
            cos_sb = sb(s2, "cos_sb", [P, TILES, HS])
            sin_sb = sb(s2, "sin_sb", [P, TILES, HS])
            qk_in = sb(s2, "qk_in", [P, 2, 2 * P])
            qk_cos = sb(s2, "qk_cos", [P, 2 * P])
            qk_rot = sb(s2, "qk_rot", [P, 2, 2 * P])
            rest = sb(s2, "rest", [P, 2, 2, P])
            mask = sb(s2, "mask", [P, QB])
            strip_max = sb(s2, "strip_max", [P, GH, TILES, CHUNKS])
            neg_max = sb(s2, "neg_max", [P, 2, GH, TPC])
            mparts = sb(s2, "mparts", [GH * TPC, 2, SPLITS, P], BF16)
            mrest = sb(s2, "mrest", [GH * TPC, P])
            o_sb = sb(s2, "o_sb", [P, 2, QB])
            recip = sb(s2, "recip", [P, TPC * GH])
            y_sb = sb(s2, "y_sb", [P, 2, TPC * GH * HS])
            ps_s = pb(s2, "ps_s", [P, RING, QB])
            ps_m = pb(s2, "ps_m", [P, RING, QB])
            ps_o = pb(s2, "ps_o", [P, QB])
            ps_j = pb(s2, "ps_j", [P, QB])

        with ExitStack() as s3:
            h1 = sb(s3, "h1", [P, 2, 2, CT, QB])
            h2 = sb(s3, "h2", [P, 2, 2, QB])
            h3 = sb(s3, "h3", [P, QB])
            th = sb(s3, "th", [P, 2, QB])
            coup = sb(s3, "coup", [P, 2, QB])
            prod = sb(s3, "prod", [P, 2, CT, QB])
            y_in = sb(s3, "y_in", [P, 2, TPC, CT, P])
            x_res = sb(s3, "x_res", [P, 2, TPC, C])
            yT = sb(s3, "yT", [P, 2, CT, P])
            res = sb(s3, "res", [P, 2, TPC, C])
            with ExitStack() as s4:
                ps_1 = pb(s4, "ps_1", [P, 2, QB])
                ps_2 = pb(s4, "ps_2", [P, 2, QB])
                ps_3 = pb(s4, "ps_3", [P, QB])
                ps_4 = pb(s4, "ps_4", [P, 2, QB])
                ps_g = pb(s4, "ps_g", [P, QB])
            with ExitStack() as s4:
                ps_t = pb(s4, "ps_t", [P, 2, QB])
                ps_y = pb(s4, "ps_y", [P, 2, QB])

        x_loaded = [sem(f"x_loaded{k}") for k in range(NT // TPC)]
        ident_loaded, weights_loaded, rope_loaded = sem("ident_loaded"), sem("weights_loaded"), sem("rope_loaded")
        stats_done, var_done, std_done, rstd_done = sem("stats_done"), sem("var_done"), sem("std_done"), sem("rstd_done")
        xn_ready, xt_ready, xt_copied = sem("xn_ready"), sem("xt_ready"), sem("xt_copied")
        set_up, ones_set = sem("set_up"), sem("ones_set")
        w_loaded = sem("w_loaded")
        win_loaded = [sem("win_loaded0"), sem("win_loaded1")]
        job_ready = sem("job_ready")
        v_ready, y_ready = sem("v_ready"), sem("y_ready")
        qk_ready, cos_done, rot_done = sem("qk_ready"), sem("cos_done"), sem("rot_done")
        hi_ready, rest_ready, mid_done, parts_ready = sem("hi_ready"), sem("rest_ready"), sem("mid_done"), sem("parts_ready")
        stack_loaded = [sem("stack_loaded0"), sem("stack_loaded1")]
        v_loaded = [sem("v_loaded0"), sem("v_loaded1")]
        max_ready, max_used = sem("max_ready"), sem("max_used")
        neg_ready, mhi_ready, mrest_ready, mmid_ready, mparts_ready = (sem(n) for n in (
            "neg_ready", "mhi_ready", "mrest_ready", "mmid_ready", "mparts_ready"))
        shift_loaded = [sem(f"shift_loaded{c}") for c in range(CHUNKS)]
        scores_ready, exp_done, mask_done, pv_done = sem("scores_ready"), sem("exp_done"), sem("mask_done"), sem("pv_done")
        o_copied, o_turned = sem("o_copied"), sem("o_turned")
        y_stored = [sem("y_stored0"), sem("y_stored1")]
        prep = sem("prep")
        l1_done, l2_done, l3_done, l4_done = sem("l1_done"), sem("l2_done"), sem("l3_done"), sem("l4_done")
        g1_done, g2_done, g3_done, th_done = sem("g1_done"), sem("g2_done"), sem("g3_done"), sem("th_done")
        coup_done, prod_done, upd_done = sem("coup_done"), sem("prod_done"), sem("upd_done")
        glob_mm, glob_act, glob_base = sem("glob_mm"), sem("glob_act"), sem("glob_base")
        yx_loaded = [sem("yx_loaded0"), sem("yx_loaded1")]
        yt_ready, yt_copied, sum_ready, res_ready = sem("yt_ready"), sem("yt_copied"), sem("sum_ready"), sem("res_ready")
        out_stored = [sem("out_stored0"), sem("out_stored1")]

        def column(v):
            return v.rearrange("(p o) -> p o", o=1)

        weights = [
            (wp_sb[:], wp.rearrange("(c p) n -> p c n", p=P)), (bp_sb[:], bp),
            (w1[:], ffn["cn_w1"].rearrange("(c p) n -> p c n", p=P)), (b1[:], ffn["cn_b1"]),
            (w2[:], ffn["cn_w2"].rearrange("(c p) n -> p c n", p=P)), (b2[:], column(ffn["cn_b2"])),
            (w3[:], ffn["cn_w3"]), (b3[0:H3], column(ffn["cn_b3"])), (b3[H3:P], column(ffn["cn_b3"])),
            (w4[0:H3], ffn["cn_w4"]), (w4[H3:P], ffn["cn_w4"]),
            (b4[:], ffn["cn_b4"].partition_broadcast(P)),
            (gw1[:], ffn["gc_w1"].rearrange("(c p) n -> p c n", p=P)), (gb1[:], column(ffn["gc_b1"])),
            (gw2[:], ffn["gc_w2"]), (gb2[:], column(ffn["gc_b2"])),
            (gw3[:], ffn["gc_w3"]), (gb3[:], ffn["gc_b3"].partition_broadcast(P)),
            (ar[:], ffn["adaptive_range"].partition_broadcast(P)),
        ]
        PREP = 7

        def rounds(eng, body):
            with eng.Fori(0, NI - 1) as i:
                body(i, LOOP_JOBS, False)
            body(NI - 1, LAST_JOBS, True)

        def jobs_before(i, jobs, s):
            return EARLY_JOBS + i * JOBS_A_ROUND + sum(map(len, jobs[:s]))

        def unit_at(i, s):
            return (i + 1) * A_ROUND + (EARLY_UNITS - A_ROUND + UNITS[s])

        def spread(units):
            n, places = len(units), GH + 2
            cut = [n * k // places for k in range(places + 1)]
            return [units[a:b] for a, b in zip(cut, cut[1:])]

        DVE_AHEAD = 1

        def wait_alone(eng, semaphore, value):
            eng.wait_ge(semaphore, value)
            eng.nop(nofuse=True)

        block = ctx.enter_context(nc.Block())

        @block.sync
        def _(sp):
            for k in range(NT // TPC):
                sp.dma_start(x_in[:, k * TPC:(k + 1) * TPC, :],
                             x_tiles[:, k * TPC:(k + 1) * TPC, :]).then_inc(x_loaded[k], 16)
                if k == 0:
                    sp.dma_start(ident[:], ident_in).then_inc(ident_loaded, 16)
            for dst, src in weights:
                sp.dma_start(dst, src).then_inc(weights_loaded, 16)

            def load_weights(r):
                sp.dma_start(wcur[:], wqkv[bass.ds(r, 1), :, :].rearrange("i (c p) n -> p (i c) n", p=P)
                             ).then_inc(w_loaded, 16)
                sp.dma_start(bcur[:], bqkv[bass.ds(r, 1), :, :].rearrange("i p n -> (i p) n")).then_inc(w_loaded, 16)

            def load_window(r, cc):
                sp.dma_start(xwin[:, cc % 2], xnT[:, :, bass.ds((r // CT) * T + cc * QB, QB)]
                             ).then_inc(win_loaded[cc % 2], 16)

            def load_stack(g):
                heads = slice(HS * GH * g, HS * GH * (g + 1))
                for side, st in ((0, qst), (1, kst)):
                    for n, pair in enumerate(SLOTS):
                        sp.dma_start(st[g][HS * n:HS * (n + 1)],
                                     parts[heads, side, pair[side], :]).then_inc(stack_loaded[g], 16)

            def load_v(g):
                sp.dma_start(vcur[g][:].rearrange("p t h d -> p (t h d)"),
                             vnext[:, g].rearrange("p t h d -> p (t h d)")).then_inc(v_loaded[g], 16)

            def load_shift(g, c):
                for p in range(SPLITS):
                    for h in range(GH):
                        sp.dma_start(qst[g % GROUPS][SHIFT + p:SHIFT + p + 1, h, c * QB:(c + 1) * QB],
                                     mparts[TPC * h:TPC * (h + 1), c % 2, p, :]).then_inc(shift_loaded[c], 16)

            sp.wait_ge(xt_copied, CT * NT // TPC)
            sp.dma_start(cos_sb[:], cos).then_inc(rope_loaded, 16)
            sp.dma_start(sin_sb[:], sin).then_inc(rope_loaded, 16)
            load_weights(0)
            for cc in range(CHUNKS):
                if cc >= 2:
                    sp.wait_ge(qk_ready, TPC * (cc - 1))
                load_window(0, cc)
            sp.wait_ge(parts_ready, TILES)
            load_stack(0)
            sp.wait_ge(v_ready, TILES)
            load_v(0)
            n = 0
            for _, k in EARLY_STRIPS:
                c = last_of_chunk(k)
                if c is not None:
                    n += 1
                    sp.wait_ge(mparts_ready, n)
                    load_shift(0, c)

            def store(k):
                sp.wait_ge(res_ready, TPC * (k + 1))
                sp.dma_start(out_tiles[:, k * TPC:(k + 1) * TPC, :], res[:, k % 2]).then_inc(out_stored[k % 2], 16)

            def body(i, jobs, last):
                if not last:
                    sp.wait_ge(v_ready, (i + 1) * TILES)
                    load_weights(i + 1)
                    for cc in (0, 1):
                        load_window(i + 1, cc)
                sp.wait_ge(scores_ready, i * A_ROUND + GH)
                load_stack(1)
                pending = []
                for s in range(BODY + 1):
                    if s == 1:
                        sp.wait_ge(pv_done, i * BODY + 1)
                        load_v(1)
                    for job in pending:
                        if job[0] == "shift":
                            sp.wait_ge(mparts_ready, i * GROUPS * CHUNKS + CHUNKS * job[1] + job[2] + 1)
                            load_shift(job[1], job[2])
                        elif job[0] == "out":
                            store_y(i, job[1])
                        elif job[0] == "proj" and job[1] in (TPC - 1, 2 * TPC - 1):
                            cc = job[1] // TPC + 2
                            sp.wait_ge(qk_ready, (i + 1) * TILES + TPC * (cc - 1))
                            load_window(i + 1, cc)
                        elif job == ("turn", TILES - 1):
                            sp.wait_ge(scores_ready, i * A_ROUND + GH * NS)
                            sp.wait_ge(parts_ready, (i + 2) * TILES)
                            load_stack(0)
                            sp.wait_ge(pv_done, i * BODY + NS)
                            load_v(0)
                    pending = jobs[s]
                for job in pending:
                    store_y(i, job[1])

            def store_y(i, n):
                sp.wait_ge(y_ready, i * ENDS[BODY] + n + 2)
                g, c = divmod(n, CHUNKS)
                sp.dma_start(
                    y_dram[bass.ds(i, 1), c * QB:(c + 1) * QB, g * GH * HS:(g + 1) * GH * HS]
                    .rearrange("i (t p) d -> p (i t) d", p=P),
                    y_sb[:, n % 2].rearrange("p (t d) -> p t d", t=TPC)).then_inc(y_stored[n % 2], 16)

            rounds(sp, body)

            for p in range(2):
                sp.wait_ge(y_stored[p], NI * ENDS[BODY] // 2 * 16 + 1)
            sp.wait_ge(pv_done, NI * BODY)
            for k in range(NT // TPC):
                if k >= 2:
                    sp.wait_ge(res_ready, TPC * (k - 1))
                b, c = divmod(k, CHUNKS)
                for half in range(CT):
                    sp.dma_start(y_in[:, k % 2, :, half, :], y_dram[CT * b + half, c * QB:(c + 1) * QB, :]
                                 .rearrange("(t p) d -> p t d", p=P)).then_inc(yx_loaded[k % 2], 16)
                sp.dma_start(x_res[:, k % 2], x_tiles[:, k * TPC:(k + 1) * TPC, :]).then_inc(yx_loaded[k % 2], 16)
                if k >= 1:
                    store(k - 1)
            store(NT // TPC - 1)
            for p in range(2):
                sp.wait_ge(out_stored[p], NT // TPC // 2 * 16)

        @block.gpsimd
        def _(pool):
            nc.gpsimd.memset(mask[:], 0.0).then_inc(set_up, 1)
            pool.wait_ge(xt_copied, CT * NT // TPC)
            pool.wait_ge(set_up, 1)
            nc.gpsimd.affine_select(out=mask[:, QB - P:], in_=mask[:, QB - P:], pattern=[[-1, P]],
                                    compare_op=ALU.is_ge, fill=NEG, base=0,
                                    channel_multiplier=1).then_inc(set_up, 1)
            pool.wait_ge(rope_loaded, 32)

            def rotate(r, t):
                n = r * TILES + t
                src, dst, cosines = (a.rearrange("p (g d h) -> p g d h", d=HS, h=GH) for a in (
                    qk_in[:, t % 2], qk_rot[:, t % 2], qk_cos[:]))

                def table(tab, a, step):
                    return tab[:, t:t + 1, a::step].rearrange("p g (d h) -> p g d h", h=1).broadcast_to(
                        [P, 2 * GROUPS, HS // step, GH])

                if not (isinstance(n, int) and n == 0):
                    pool.wait_ge(rot_done, n)
                pool.wait_ge(qk_ready, n + 1)
                nc.gpsimd.tensor_tensor(cosines, src,
                                        table(cos_sb, 0, 1), ALU.mult).then_inc(cos_done, 1)
                if not (isinstance(r, int) and r == 0 and t < 2):
                    pool.wait_ge(rest_ready, n - 1)
                for a in (0, 1):
                    nc.gpsimd.tensor_tensor(dst[:, :, a::2, :], src[:, :, 1 - a::2, :],
                                            table(sin_sb, a, 2), ALU.mult).then_inc(cos_done, 1)
                pool.wait_ge(cos_done, 3 * (n + 1))
                nc.gpsimd.tensor_tensor(qk_rot[:, t % 2], qk_rot[:, t % 2], qk_cos[:],
                                        ALU.add).then_inc(rot_done, 1)

            def split(r, t):
                n = r * TILES + t
                wait_alone(pool, rest_ready, n + 1)
                at = slice(t * P, (t + 1) * P)
                nc.gpsimd.tensor_copy(parts[:, :, 1, at], rest[:, t % 2]).then_inc(mid_done, 1)
                pool.wait_ge(mid_done, n + 1)
                nc.gpsimd.tensor_tensor(parts[:, :, 2, at], rest[:, t % 2], parts[:, :, 1, at],
                                        ALU.subtract).then_inc(parts_ready, 1)

            def mask_step(i, s):
                lo = STEPS[s % NS][2]
                wait_alone(pool, exp_done, i * A_ROUND + GH * (s + 1))
                blockp = probs[:, s % 2, :, lo:lo + P]
                nc.gpsimd.affine_select(out=blockp, in_=blockp, pattern=[[0, GH], [1, P]],
                                        compare_op=ALU.is_ge, fill=0.0, base=0,
                                        channel_multiplier=-1).then_inc(mask_done, 1)

            for job, t in project_order():
                rotate(0, t) if job == "proj" else split(0, t)
            mask_step(0, 0)

            def body(i, jobs, last):
                for s in range(BODY):
                    if s + 1 < BODY:
                        if diagonal(s + 1):
                            mask_step(i, s + 1)
                    elif not last:
                        mask_step(i + 1, 0)
                    for job in jobs[s]:
                        if job[0] == "proj":
                            rotate(i + 1, job[1])
                        elif job[0] == "turn":
                            split(i + 1, job[1])

            rounds(pool, body)

        @block.scalar
        def _(act):
            act.wait_ge(var_done, 1)
            nc.scalar.activation(std[:], std[:], ACT.Sqrt).then_inc(std_done, 1)
            for k in range(NT // TPC):
                for c in range(CT):
                    act.wait_ge(xt_ready, k * CT + c + 1)
                    nc.scalar.activation(xnT[:, c, k * QB:(k + 1) * QB], ps_x[:, k % 2, c, :],
                                         ACT.Copy).then_inc(xt_copied, 1)

            def exps(i, s):
                lo = STEPS[s % NS][2]
                for h in range(GH):
                    n = GH * s + h
                    act.wait_ge(scores_ready, i * A_ROUND + n + 1)
                    if h == 0 and s >= 2:
                        act.wait_ge(pv_done, i * BODY + s - 1)
                    elif h == 0 and s == 0 and not (isinstance(i, int) and i == 0):
                        act.wait_ge(pv_done, i * BODY - 1)
                    nc.scalar.activation(probs[:, s % 2, h, lo:], ps_s[:, n % RING, lo:], ACT.Exp,
                                         scale=SCALE).then_inc(exp_done, 1)

            def high(r, t, number):
                act.wait_ge(job_ready, number + 1)
                if t == 0 and not (isinstance(r, int) and r == 0):
                    for g in range(GROUPS):
                        act.wait_ge(stack_loaded[g], r * STACK_DMAS * 16)
                nc.scalar.activation(parts[:, :, 0, t * P:(t + 1) * P],
                                     ps_j[:, 0:2 * P].rearrange("p (a n) -> p a n", a=2),
                                     ACT.Copy).then_inc(hi_ready, 1)

            def shift_high(g, c, number):
                act.wait_ge(job_ready, number + 1)
                if c >= 2:
                    act.wait_ge(shift_loaded[c - 2], (g + 1) * SHIFT_DMAS * 16)
                elif not (isinstance(g, int) and g == 0):
                    act.wait_ge(shift_loaded[c + 2], g * SHIFT_DMAS * 16)
                nc.scalar.activation(mparts[:, c % 2, 0, :], ps_j[0:GH * TPC, 0:P],
                                     ACT.Copy).then_inc(mhi_ready, 1)

            def copy_out(i, s):
                n = ENDS[s]
                act.wait_ge(pv_done, i * BODY + s + 1)
                act.wait_ge(o_turned, i * ENDS[BODY] + max(n - 1, 0) + 1)
                nc.scalar.activation(o_sb[:, n % 2], ps_o[:], ACT.Copy).then_inc(o_copied, 1)

            for number, (job, t) in enumerate(project_order()):
                if job == "turn":
                    high(0, t, number)
            number = len(project_order())
            for _, k in EARLY_STRIPS:
                c = last_of_chunk(k)
                if c is not None:
                    shift_high(0, c, number)
                    number += 1
            exps(0, 0)

            def body(i, jobs, last):
                for s in range(BODY + 1):
                    if s + 1 < BODY:
                        exps(i, s + 1)
                    elif s + 1 == BODY and not last:
                        exps(i + 1, 0)
                    for n, job in enumerate(jobs[s]):
                        number = jobs_before(i, jobs, s) + n
                        if job[0] == "turn":
                            high(i + 1, job[1], number)
                        elif job[0] == "shift":
                            shift_high(i * GROUPS + job[1], job[2], number)
                    if s < BODY and ends_block(s):
                        copy_out(i, s)

            rounds(act, body)

            for p in range(2):
                act.wait_ge(y_stored[p], NI * ENDS[BODY] // 2 * 16 + 1)

            def gelu(out_, in_, bias, done):
                nc.scalar.activation(out_, in_, ACT.Gelu, bias=bias).then_inc(done, 1)

            def gelu_1(n, blk):
                for m in range(CT):
                    u = 4 * n + CT * blk + m
                    act.wait_ge(l1_done, u + 1)
                    if n >= 2:
                        act.wait_ge(l2_done, 2 * (n - 2) + blk + 1)
                    gelu(h1[:, n % 2, blk, m, :], ps_1[:, m, :], b1[:, m:m + 1], g1_done)

            def global_net(stage):
                act.wait_ge(glob_mm, stage + 1)
                if stage == 0:
                    gelu(gh1[:], ps_g[:, 0:B], gb1[:, 0:1], glob_act)
                elif stage == 1:
                    gelu(gh2[:], ps_g[0:H3, 0:B], gb2[:, 0:1], glob_act)
                else:
                    nc.scalar.activation(gtanh[:], ps_g[:, 0:B], ACT.Tanh, bias=gb3[:, 0:1],
                                         scale=0.5).then_inc(glob_act, 1)

            act.wait_ge(weights_loaded, 16 * len(weights))
            act.wait_ge(prep, PREP)
            for n in range(CYCLES * PAIRS + 2):
                if n < CYCLES * PAIRS:
                    gelu_1(n, 0)
                if n >= 2:
                    m = n - 2
                    act.wait_ge(l3_done, m + 1)
                    if m >= 1:
                        act.wait_ge(l4_done, 2 * m)
                    gelu(h3[:], ps_3[:], b3[:, 0:1], g3_done)
                if n < CYCLES * PAIRS:
                    gelu_1(n, 1)
                if n >= 2:
                    for blk in range(2):
                        act.wait_ge(l4_done, 2 * m + blk + 1)
                        if m >= 1:
                            act.wait_ge(coup_done, 2 * (m - 1) + blk + 1)
                        nc.scalar.activation(th[:, blk, :], ps_4[:, blk, :], ACT.Tanh, bias=b4[:, 0:1],
                                             scale=0.5).then_inc(th_done, 1)
                if n < 3:
                    global_net(n)
                if 1 <= n <= CYCLES * PAIRS:
                    m = n - 1
                    for blk in range(2):
                        act.wait_ge(l2_done, 2 * m + blk + 1)
                        if m >= 2:
                            act.wait_ge(l3_done, m - 1)
                        gelu(h2[:, m % 2, blk, :], ps_2[:, blk, :], b2[:, 0:1], g2_done)

            for t in range(NT):
                act.wait_ge(yt_ready, t + 1)
                if t >= 2:
                    act.wait_ge(sum_ready, t - 1)
                nc.scalar.activation(yT[:, t % 2], ps_t[:, t % 2, 0:C].rearrange("p (c n) -> p c n", c=CT),
                                     ACT.Copy).then_inc(yt_copied, 1)

        @block.vector
        def _(dve):
            for k in range(NT // TPC):
                dve.wait_ge(x_loaded[k], 16)
                for t in range(k * TPC, (k + 1) * TPC):
                    nc.vector.bn_stats(stats[:, t, :], x_in[:, t, :]).then_inc(stats_done, 1)
            for t in range(NT):
                dve.wait_ge(stats_done, t + 1)
                nc.vector.bn_aggr(meanvar[:, t, :], stats[:, t, :]).then_inc(stats_done, 1)
            dve.wait_ge(stats_done, 2 * NT)
            nc.vector.tensor_scalar(std[:], meanvar[:, :, 1], EPS, None, ALU.add).then_inc(var_done, 1)
            dve.wait_ge(std_done, 1)
            nc.vector.reciprocal(rstd[:], std[:]).then_inc(rstd_done, 1)
            dve.wait_ge(rstd_done, 1)
            for t in range(NT):
                nc.vector.tensor_scalar(x_in[:, t, :], x_in[:, t, :], meanvar[:, t, 0:1], rstd[:, t:t + 1],
                                        ALU.subtract, ALU.mult).then_inc(xn_ready, 1)

            dve.wait_ge(weights_loaded, 16 * len(weights))
            nc.vector.memset(sign[0:H3], 1.0).then_inc(prep, 1)
            nc.vector.memset(sign[H3:P], -1.0).then_inc(prep, 1)
            nc.vector.memset(w4_wide[:], 0.0).then_inc(prep, 1)
            dve.wait_ge(prep, 3)
            nc.vector.tensor_scalar(b4[:], b4[:], 0.5, None, ALU.mult).then_inc(prep, 1)
            nc.vector.tensor_scalar(gb3[:], gb3[:], 0.5, None, ALU.mult).then_inc(prep, 1)
            for blk in range(2):
                rows = slice(H3 * blk, H3 * (blk + 1))
                nc.vector.tensor_scalar(w4_wide[rows, blk, :], w4_wide[rows, blk, :], w4[rows, 0:1], None,
                                        ALU.add).then_inc(prep, 1)
            nc.vector.tensor_scalar(swing[:], ar[:], sign[:, 0:1], 0.3, ALU.mult, ALU.mult).then_inc(glob_base, 1)
            nc.vector.memset(gw3_wide[:], 0.0).then_inc(glob_base, 1)
            dve.wait_ge(glob_base, 2)
            nc.vector.tensor_scalar(gw3_wide[:], gw3_wide[:], gw3[:, 0:1], None, ALU.add).then_inc(glob_base, 1)

            dve.wait_ge(xt_copied, CT * NT // TPC)
            for g in range(GROUPS):
                nc.vector.memset(kst[g][SHIFT:KROWS], 1.0).then_inc(ones_set, 1)
            nc.vector.memset(vnext[:], 1.0).then_inc(ones_set, 1)
            nc.vector.memset(ps_o[:], 0.0).then_inc(ones_set, 1)
            dve.wait_ge(ones_set, 4)
            for free, buf in ((o_turned, o_sb[:, 0, 0:1]), (y_ready, recip[:, 0:1]),
                              (y_stored[0], y_sb[:, 0, 0:1]), (y_stored[1], y_sb[:, 1, 0:1])):
                nc.vector.memset(buf, 0.0).then_inc(free, 1)

            def project(r, t, number):
                n = r * TILES + t
                first = isinstance(r, int) and r == 0
                dve.wait_ge(job_ready, number + 1)
                if not (first and t < 2):
                    dve.wait_ge(rot_done, n - 1)
                nc.vector.tensor_tensor(qk_in[:, t % 2], ps_j[:, 0:2 * P], bcur[:, 0:2 * P],
                                        ALU.add).then_inc(qk_ready, 1)
                if t == 0 and not first:
                    for g in range(GROUPS):
                        dve.wait_ge(v_loaded[g], r * 16)
                nc.vector.tensor_tensor(vnext[:, :, t, :, 0:HS],
                                        ps_j[:, 2 * P:3 * P].rearrange("p (g h d) -> p g h d", g=GROUPS, h=GH),
                                        bcur[:, 2 * P:3 * P].rearrange("p (g h d) -> p g h d", g=GROUPS, h=GH),
                                        ALU.add).then_inc(v_ready, 1)

            def remainder(r, t):
                n = r * TILES + t
                dve.wait_ge(hi_ready, n + 1)
                if not (isinstance(r, int) and r == 0 and t < 2):
                    dve.wait_ge(parts_ready, n - 1)
                nc.vector.tensor_tensor(rest[:, t % 2], ps_j[:, 0:2 * P].rearrange("p (a n) -> p a n", a=2),
                                        parts[:, :, 0, t * P:(t + 1) * P], ALU.subtract).then_inc(rest_ready, 1)

            def strip(g, k, h, unit, place):
                t, kb, w = STRIPS[k]
                at = strip_max[:, h, t, kb:kb + 1]
                scores = ps_m[:, place % RING, 0:w]
                if kb == t // TPC:
                    dve.wait_ge(set_up, 2)
                    wait_alone(dve, max_ready, unit + 1)
                else:
                    dve.wait_ge(max_ready, unit + 1)
                if kb == t // TPC:
                    nc.vector.tensor_tensor_reduce(scores, scores, mask[:, QB - w:], 1.0, NEG,
                                                   ALU.add, ALU.max, at).then_inc(max_used, 1)
                else:
                    nc.vector.tensor_reduce(at, scores, AX_X, ALU.max).then_inc(max_used, 1)

            def chunk_max(c, units):
                dve.wait_ge(max_used, units)
                nc.vector.tensor_reduce(neg_max[:, c % 2], strip_max[:, :, TPC * c:TPC * (c + 1), 0:c + 1],
                                        AX_X, ALU.max, negate=True).then_inc(neg_ready, 1)

            def shift(c, n):
                m = mparts[:, c % 2]
                dve.wait_ge(mhi_ready, n + 1)
                nc.vector.tensor_tensor(mrest[:], ps_j[0:GH * TPC, 0:P], m[:, 0, :],
                                        ALU.subtract).then_inc(mrest_ready, 1)
                dve.wait_ge(mrest_ready, n + 1)
                nc.vector.tensor_copy(m[:, 1, :], mrest[:]).then_inc(mmid_ready, 1)
                dve.wait_ge(mmid_ready, n + 1)
                nc.vector.tensor_tensor(m[:, 2, :], mrest[:], m[:, 1, :], ALU.subtract).then_inc(mparts_ready, 1)

            def normalise(i, n, number):
                turned = ps_j[:].rearrange("p (a d) -> p a d", d=2 * HS)
                dve.wait_ge(job_ready, number + 1)
                nc.vector.reciprocal(recip[:].rearrange("p (a d) -> p a d", d=1),
                                     turned[:, :, HS:VW]).then_inc(o_turned, 1)
                dve.wait_ge(o_turned, i * ENDS[BODY] + n + 2)
                dve.wait_ge(y_stored[n % 2], (i * (ENDS[BODY] // 2) + n // 2) * 16 + 1)
                nc.vector.tensor_tensor(y_sb[:, n % 2].rearrange("p (a d) -> p a d", d=HS), turned[:, :, 0:HS],
                                        recip[:].rearrange("p (a d) -> p a d", d=1)
                                        .broadcast_to([P, TPC * GH, HS]), ALU.mult).then_inc(y_ready, 1)

            for number, (job, t) in enumerate(project_order()):
                if job == "proj":
                    project(0, t, number)
                else:
                    remainder(0, t)
            unit = 0
            for g, k in EARLY_STRIPS:
                for h in range(GH):
                    strip(g, k, h, unit, A_ROUND - EARLY_UNITS + unit)
                    unit += 1
                c = last_of_chunk(k)
                if c is not None:
                    chunk_max(c, unit)
                    shift(c, c)

            def read_jobs(i, jobs, s):
                for n, job in enumerate(jobs[s] if s >= 0 else []):
                    number = jobs_before(i, jobs, s) + n
                    if job[0] == "proj":
                        project(i + 1, job[1], number)
                    elif job[0] == "turn":
                        remainder(i + 1, job[1])
                    elif job[0] == "shift":
                        shift(job[2], (i * GROUPS + job[1]) * CHUNKS + job[2])
                    else:
                        normalise(i, job[1], number)

            def body(i, jobs, last):
                for s in range(BODY + 1):
                    units = [(g, k, h) for g, k in (strips_at(s) if s < BODY else [])
                             if not (last and g == GROUPS) for h in range(GH)]
                    for n, (g, k, h) in enumerate(units):
                        if n == DVE_AHEAD:
                            read_jobs(i, jobs, s - 1)
                        strip(g, k, h, unit_at(i, s) + n, UNITS[s] + n)
                        c = last_of_chunk(k)
                        if c is not None and h == GH - 1:
                            chunk_max(c, unit_at(i, s) + n + 1)
                    if len(units) <= DVE_AHEAD:
                        read_jobs(i, jobs, s - 1)
                read_jobs(i, jobs, BODY)

            rounds(dve, body)

            for p in range(2):
                dve.wait_ge(y_stored[p], NI * ENDS[BODY] // 2 * 16 + 1)
            for c in range(CT):
                nc.vector.tensor_reduce(xsum[:, c, :], xnT[:, c, :].rearrange("p (b t) -> p b t", b=B), AX_X,
                                        ALU.add).then_inc(glob_base, 1)
            dve.wait_ge(glob_base, 3 + CT)
            nc.vector.tensor_scalar(xsum[:], xsum[:], 1.0 / T, None, ALU.mult).then_inc(glob_base, 1)
            dve.wait_ge(glob_act, 3)
            nc.vector.tensor_scalar(base[:], gtanh[:], ar[:, 0:1], 0.7, ALU.mult, ALU.mult).then_inc(glob_base, 1)
            dve.wait_ge(glob_base, 5 + CT)
            nc.vector.tensor_scalar(base[:], base[:], 0.1, sign[:, 0:1], ALU.add, ALU.mult).then_inc(glob_base, 1)
            dve.wait_ge(glob_base, 6 + CT)

            for m in range(CYCLES * PAIRS):
                for blk in range(2):
                    n = 2 * m + blk
                    p = m % PAIRS
                    b = p * B // PAIRS
                    tok = slice((2 * p + blk) * QB, (2 * p + blk + 1) * QB)
                    dve.wait_ge(th_done, n + 1)
                    nc.vector.tensor_scalar(coup[:, blk, :], th[:, blk, :], swing[:, 0:1], base[:, b:b + 1],
                                            ALU.mult, ALU.add).then_inc(coup_done, 1)
                    dve.wait_ge(coup_done, n + 1)
                    for c in range(CT):
                        nc.vector.tensor_tensor(prod[:, blk, c, :], coup[:, blk, :], xnT[:, 1 - c, tok],
                                                ALU.mult).then_inc(prod_done, 1)
                    dve.wait_ge(prod_done, 2 * n + 2)
                    for c, op in ((0, ALU.add), (1, ALU.subtract)):
                        if m < (CYCLES - 1) * PAIRS:
                            nc.vector.tensor_tensor(xnT[:, c, tok], xnT[:, c, tok], prod[:, blk, c, :],
                                                    op).then_inc(upd_done, 1)
                        else:
                            nc.vector.scalar_tensor_tensor(xnT[:, c, tok], xnT[:, c, tok], bp_sb[:, c:c + 1],
                                                           prod[:, blk, c, :], ALU.add, op).then_inc(upd_done, 1)

            for t in range(NT):
                k = t // TPC
                dve.wait_ge(sum_ready, t + 1)
                dve.wait_ge(yx_loaded[k % 2], (k // 2 + 1) * 48)
                if t % TPC == 0 and k >= 2:
                    dve.wait_ge(out_stored[k % 2], (k // 2) * 16)
                nc.vector.tensor_tensor(res[:, k % 2, t % TPC, :], ps_y[:, t % 2, 0:C], x_res[:, k % 2, t % TPC, :],
                                        ALU.add).then_inc(res_ready, 1)

        @block.tensor
        def _(pe):
            pe.wait_ge(ident_loaded, 16)
            for k in range(NT // TPC):
                if k >= 2:
                    pe.wait_ge(xt_copied, CT * (k - 1))
                pe.wait_ge(xn_ready, TPC * (k + 1))
                for c in range(CT):
                    for t in range(TPC):
                        last = nc.tensor.transpose(ps_x[:, k % 2, c, t * P:(t + 1) * P],
                                                   x_in[:, k * TPC + t, c * P:(c + 1) * P], ident[:])
                    last.then_inc(xt_ready, 1)

            def bank_free(r, i, job, early_chunks=0):
                if job[0] == "proj":
                    pe.wait_ge(v_ready, r * TILES + job[1] + 1)
                elif job[0] == "turn":
                    pe.wait_ge(rest_ready, r * TILES + job[1] + 1)
                elif job[0] == "shift":
                    pe.wait_ge(mrest_ready, (i * GROUPS + job[1]) * CHUNKS + job[2] + 1)
                else:
                    pe.wait_ge(y_ready, i * ENDS[BODY] + job[1] + 2)

            def project(r, t):
                if t == 0:
                    pe.wait_ge(w_loaded, (r + 1) * 32)
                cc = t // TPC
                if t % TPC == 0:
                    pe.wait_ge(win_loaded[cc % 2], (r * 2 + cc // 2 + 1) * 16)
                at = slice(t % TPC * P, (t % TPC + 1) * P)
                for c in range(CT):
                    last = nc.tensor.matmul(ps_j[:, 0:QKV], xwin[:, cc % 2, c, at], wcur[:, c, :],
                                            start=(c == 0), stop=(c == CT - 1))
                last.then_inc(job_ready, 1)

            def turn(r, t):
                pe.wait_ge(rot_done, r * TILES + t + 1)
                for side in range(2):
                    last = nc.tensor.transpose(ps_j[:, side * P:(side + 1) * P],
                                               qk_rot[:, t % 2, side * P:(side + 1) * P], ident[:])
                last.then_inc(job_ready, 1)

            def turn_max(n, c):
                pe.wait_ge(neg_ready, n + 1)
                nc.tensor.transpose(ps_j[0:GH * TPC, 0:P], neg_max[:, c % 2].rearrange("p h t -> p (h t)"),
                                    ident[:]).then_inc(job_ready, 1)

            def turn_out(i, n):
                pe.wait_ge(o_copied, i * ENDS[BODY] + n + 1)
                for t in range(TPC):
                    last = nc.tensor.transpose(ps_j[:, t * P:(t + 1) * P], o_sb[:, n % 2, t * P:(t + 1) * P],
                                               ident[:])
                last.then_inc(job_ready, 1)

            def strip(g, k, h, unit, place):
                t, kb, w = STRIPS[k]
                buf = g % GROUPS
                if not (isinstance(unit, int) and unit < RING):
                    pe.wait_ge(max_used, unit + 1 - ring_distance(place))
                nc.tensor.matmul(ps_m[:, place % RING, 0:w], qst[buf][0:ROWS, h, t * P:(t + 1) * P],
                                 kst[buf][0:ROWS, h, kb * QB:kb * QB + w], start=True, stop=True
                                 ).then_inc(max_ready, 1)

            def scores(i, s, h):
                g, n = divmod(s, NS)
                c, kt, lo = STEPS[n]
                if h == 0 and kt == 0:
                    pe.wait_ge(shift_loaded[c], (i * GROUPS + g + 1) * SHIFT_DMAS * 16)
                n = GH * s + h
                if not (isinstance(i, int) and i * A_ROUND + n < RING):
                    pe.wait_ge(exp_done, i * A_ROUND + n + 1 - ring_distance(n))
                nc.tensor.matmul(ps_s[:, n % RING, lo:], kst[g][0:KROWS, h, kt * P:(kt + 1) * P],
                                 qst[g][0:KROWS, h, c * QB + lo:(c + 1) * QB], start=True, stop=True
                                 ).then_inc(scores_ready, 1)

            def values(i, s):
                g, n = divmod(s, NS)
                c, kt, lo = STEPS[n]
                if diagonal(s):
                    pe.wait_ge(mask_done, i * DIAG[BODY] + DIAG[s] + 1)
                else:
                    pe.wait_ge(exp_done, i * A_ROUND + GH * (s + 1))
                if n == 0:
                    pe.wait_ge(v_loaded[g], (i + 1) * 16)
                if kt == 0 and s > 0:
                    pe.wait_ge(o_copied, i * ENDS[BODY] + ENDS[s])
                for h in range(GH):
                    last = nc.tensor.matmul(ps_o[2 * HS * h:2 * HS * h + VW, lo:], vcur[g][:, kt, h, :],
                                            probs[:, s % 2, h, lo:], start=(kt == 0),
                                            stop=(kt == TPC * (c + 1) - 1))
                last.then_inc(pv_done, 1)

            pe.wait_ge(xt_copied, CT * NT // TPC)
            pe.wait_ge(ones_set, 4)
            before = None
            for job, t in project_order():
                if before:
                    bank_free(0, 0, before)
                project(0, t) if job == "proj" else turn(0, t)
                before = (job, t)
            pe.wait_ge(stack_loaded[0], STACK_DMAS * 16)
            unit = 0
            for g, k in EARLY_STRIPS:
                for h in range(GH):
                    strip(g, k, h, unit, A_ROUND - EARLY_UNITS + unit)
                    unit += 1
                c = last_of_chunk(k)
                if c is not None:
                    bank_free(0, 0, before)
                    turn_max(c, c)
                    before = ("shift", 0, c)
            for h in range(GH):
                scores(0, 0, h)
            early = len([k for _, k in EARLY_STRIPS if last_of_chunk(k) is not None])

            def body(i, jobs, last):
                before = None
                for s in range(BODY + 1):
                    strips = [(g, k) for g, k in (strips_at(s) if s < BODY else []) if not (last and g == GROUPS)]
                    units = [(g, k, h) for g, k in strips for h in range(GH)]
                    for g, k in strips:
                        if k == 0:
                            pe.wait_ge(stack_loaded[g % GROUPS], (i + 1 + g // GROUPS) * STACK_DMAS * 16)
                    number = 0
                    for place, few in enumerate(spread(units)):
                        for g, k, h in few:
                            strip(g, k, h, unit_at(i, s) + number, UNITS[s] + number)
                            number += 1
                        if place < GH and s + 1 < BODY:
                            scores(i, s + 1, place)
                        elif place < GH and s + 1 == BODY and not last:
                            scores(i + 1, 0, place)
                        elif place == GH and s < BODY:
                            values(i, s)
                    for job in jobs[s]:
                        if before:
                            bank_free(i + 1, i, before)
                        else:
                            pe.wait_ge(v_ready, (i + 1) * TILES)
                            pe.wait_ge(rest_ready, (i + 1) * TILES)
                            pe.wait_ge(mrest_ready, i * GROUPS * CHUNKS + early)
                            pe.wait_ge(y_ready, i * ENDS[BODY] + 1)
                        if job[0] == "proj":
                            project(i + 1, job[1])
                        elif job[0] == "turn":
                            turn(i + 1, job[1])
                        elif job[0] == "shift":
                            turn_max((i * GROUPS + job[1]) * CHUNKS + job[2], job[2])
                        else:
                            turn_out(i, job[1])
                        before = job

            rounds(pe, body)

            def layer_1(n, blk):
                p = n % PAIRS
                tok = slice((2 * p + blk) * QB, (2 * p + blk + 1) * QB)
                if n >= PAIRS:
                    pe.wait_ge(upd_done, 2 * (2 * (n - PAIRS) + blk + 1))
                for m in range(CT):
                    u = 4 * n + CT * blk + m
                    if u >= 2:
                        pe.wait_ge(g1_done, u - 1)
                    for c in range(CT):
                        last = nc.tensor.matmul(ps_1[:, m, :], w1[:, c, m * P:(m + 1) * P], xnT[:, c, tok],
                                                start=(c == 0), stop=(c == CT - 1))
                    last.then_inc(l1_done, 1)

            def layer_2(n, blk):
                pe.wait_ge(g1_done, 4 * n + CT * (blk + 1))
                if n >= 1:
                    pe.wait_ge(g2_done, 2 * (n - 1) + blk + 1)
                for c in range(CT):
                    last = nc.tensor.matmul(ps_2[:, blk, :], w2[:, c, :], h1[:, n % 2, blk, c, :],
                                            start=(c == 0), stop=(c == CT - 1))
                last.then_inc(l2_done, 1)

            def layer_3(n):
                pe.wait_ge(g2_done, 2 * n + 2)
                if n >= 1:
                    pe.wait_ge(g3_done, n)
                for blk in range(2):
                    last = nc.tensor.matmul(ps_3[H3 * blk:H3 * (blk + 1), :], w3[:], h2[:, n % 2, blk, :],
                                            start=True, stop=True)
                last.then_inc(l3_done, 1)

            def layer_4(n):
                pe.wait_ge(g3_done, n + 1)
                for blk in range(2):
                    if n >= 1:
                        pe.wait_ge(th_done, 2 * (n - 1) + blk + 1)
                    nc.tensor.matmul(ps_4[:, blk, :], w4_wide[:, blk, :], h3[:], start=True,
                                     stop=True).then_inc(l4_done, 1)

            def global_net(stage):
                if stage == 0:
                    pe.wait_ge(glob_base, 4 + CT)
                    for c in range(CT):
                        last = nc.tensor.matmul(ps_g[:, 0:B], gw1[:, c, :], xsum[:, c, :], start=(c == 0),
                                                stop=(c == CT - 1))
                else:
                    pe.wait_ge(glob_act, stage)
                    if stage == 1:
                        last = nc.tensor.matmul(ps_g[0:H3, 0:B], gw2[:], gh1[:], start=True, stop=True)
                    else:
                        last = nc.tensor.matmul(ps_g[:, 0:B], gw3_wide[:], gh2[:], start=True, stop=True)
                last.then_inc(glob_mm, 1)

            pe.wait_ge(exp_done, NI * A_ROUND)
            pe.wait_ge(y_ready, NI * ENDS[BODY] + 1)
            pe.wait_ge(prep, PREP)
            for n in range(CYCLES * PAIRS + 2):
                if n < CYCLES * PAIRS:
                    layer_1(n, 0)
                if n >= 2:
                    layer_3(n - 2)
                if n < CYCLES * PAIRS:
                    layer_1(n, 1)
                if n >= 2:
                    layer_4(n - 2)
                if n < 3:
                    global_net(n)
                if 1 <= n <= CYCLES * PAIRS:
                    for blk in range(2):
                        layer_2(n - 1, blk)

            def turn_y(t):
                k = t // TPC
                if t % TPC == 0:
                    pe.wait_ge(yx_loaded[k % 2], (k // 2 + 1) * 48)
                if t >= 2:
                    pe.wait_ge(yt_copied, t - 1)
                for c in range(CT):
                    last = nc.tensor.transpose(ps_t[:, t % 2, c * P:(c + 1) * P], y_in[:, k % 2, t % TPC, c, :],
                                               ident[:])
                last.then_inc(yt_ready, 1)

            pe.wait_ge(upd_done, 4 * CYCLES * PAIRS)
            turn_y(0)
            for t in range(NT):
                if t + 1 < NT:
                    turn_y(t + 1)
                pe.wait_ge(yt_copied, t + 1)
                if t >= 2:
                    pe.wait_ge(res_ready, t - 1)
                for c in range(CT):
                    nc.tensor.matmul(ps_y[:, t % 2, 0:C], yT[:, t % 2, c, :], wp_sb[:, c, :], start=(c == 0),
                                     stop=False)
                for c in range(CT):
                    last = nc.tensor.matmul(ps_y[:, t % 2, c * P:(c + 1) * P], xnT[:, c, t * P:(t + 1) * P],
                                            ident[:], start=False, stop=(c == CT - 1))
                last.then_inc(sum_ready, 1)


_FFN = ["cn_w1", "cn_b1", "cn_w2", "cn_b2", "cn_w3", "cn_b3", "cn_w4", "cn_b4", "gc_w1", "gc_b1", "gc_w2", "gc_b2",
        "gc_w3", "gc_b3", "adaptive_range"]


def rope_tables():
    half = HS // 2
    inv_freq = (np.float32(1.0) / np.float32(10000.0) ** (np.arange(half, dtype=np.float32) * np.float32(2.0)
                                                          / np.float32(HS))).astype(np.float32)
    ang = np.arange(T, dtype=np.float32)[:, None] * inv_freq[None, :]
    cos = np.repeat(np.cos(ang), 2, axis=1)
    sin = np.stack([-np.sin(ang), np.sin(ang)], axis=-1).reshape(T, HS)
    return [np.ascontiguousarray(a.astype(np.float32).reshape(TILES, P, HS).transpose(1, 0, 2)) for a in (cos, sin)]


def by_partition(v):
    return np.ascontiguousarray(v.reshape(CT, P).T)


def kernel(**inputs):
    import concourse.bacc as bacc
    from concourse.bass_utils import run_bass_kernel_spmd

    a = {k: np.ascontiguousarray(v) for k, v in inputs.items()}
    by_head = np.arange(P)
    by_dim = by_head.reshape(GROUPS, GH, HS).transpose(0, 2, 1).reshape(P)
    halves = [[P * (i % CT) + order for order in (by_dim, by_dim, by_head)] for i in range(NI)]
    wqkv = np.stack([np.concatenate([a[f"L0_attn_W{n}"][:, h] for n, h in zip("qkv", half)], axis=1)
                     for half in halves])
    bqkv = np.stack([np.concatenate([a[f"L0_attn_b{n}"][h] for n, h in zip("qkv", half)]) for half in halves])
    cos, sin = rope_tables()
    arrays = {
        "x": a["L0_attn_x"], "wqkv": wqkv, "bqkv": np.ascontiguousarray(np.broadcast_to(bqkv[:, None], (NI, P, QKV))),
        "wp": a["L0_attn_Wp"], "bp": by_partition(a["L0_attn_bp"]), "cos": cos, "sin": sin, "ident": np.eye(P, dtype=np.float32),
    }
    for n in _FFN:
        arrays[n] = a[f"L0_ffn_{n}"]
    arrays["cn_b1"] = by_partition(arrays["cn_b1"])
    nc = bacc.Bacc("TRN2", target_bir_lowering=False, num_devices=1)
    ap = {n: nc.dram_tensor(f"{n}_dram", v.shape, F32, kind="ExternalInput").ap() for n, v in arrays.items()}
    out = nc.dram_tensor("out_dram", (B, T, C), F32, kind="ExternalOutput").ap()
    y_dram = nc.dram_tensor("y_scratch", (NI, T, P), F32, kind="Internal").ap()
    build(nc, ap["x"], ap["wqkv"], ap["bqkv"], ap["wp"], ap["bp"], ap["cos"], ap["sin"], ap["ident"],
          {n: ap[n] for n in _FFN}, out, y_dram)
    r = run_bass_kernel_spmd(nc, [{f"{n}_dram": v for n, v in arrays.items()}], core_ids=[0])
    return r.results[0]["out_dram"]
```

```python
from contextlib import ExitStack

import numpy as np

import concourse.bass as bass
from concourse import mybir

ALU = mybir.AluOpType
ACT = mybir.ActivationFunctionType
AX_X = mybir.AxisListType.X
F32 = mybir.dt.float32
BF16 = mybir.dt.bfloat16

P = 128
B, T, C, NH = 2, 2048, 256, 16
HS = C // NH
CT = C // P
NI = B * CT
GH = 4
GROUPS = 2
TILES = T // P
QB = 512
CHUNKS = T // QB
TPC = QB // P
QKV = 3 * P
SPLITS = 3
SLOTS = [(0, 0), (1, 0), (2, 0), (0, 1), (1, 1), (0, 2)]
ROWS = HS * len(SLOTS)
SHIFT = ROWS
KROWS = ROWS + SPLITS
VW = HS + 1
SCALE = float(HS) ** -0.5
NEG = -1.0e30
EPS = 1e-5
H3 = 64
CYCLES = 3
PAIRS = B * T // (2 * QB)
RING = 3
INPUTS = 4
LEAD = 72

FIRST_STRIP = TPC + 3

STEPS = [(c, kt, max(0, kt * P - c * QB)) for c in range(CHUNKS) for kt in range(TPC * (c + 1))]
STRIPS = [(t, kb, min(QB, P * (t + 1) - QB * kb)) for t in range(TILES) for kb in range(t // TPC + 1)]
NS = len(STEPS)
BODY = GROUPS * NS
BLOCKS = sum(w for _, _, w in STRIPS) // P


def strips_before(work):
    n, done = 0, 0
    while done < work:
        done += STRIPS[n % len(STRIPS)][2] // P
        n += 1
    return n


def step_work(n):
    return sum(QB - lo for _, _, lo in STEPS[:n]) // P


def strips_at(s):
    g, n = divmod(s, NS)
    a = strips_before(step_work(n) + LEAD) if n else strips_before(LEAD)
    b = strips_before(step_work(n + 1) + LEAD)
    return [(g + k // len(STRIPS), k % len(STRIPS)) for k in range(a, b)]


EARLY_STRIPS = [(0, k) for k in range(strips_before(LEAD))]


def last_of_chunk(k):
    t = STRIPS[k][0]
    last = k + 1 == len(STRIPS) or STRIPS[k + 1][0] != t
    return t // TPC if last and t % TPC == TPC - 1 else None


def round_jobs(last):
    at = [[] for _ in range(BODY + 1)]
    for s in range(BODY):
        for g, k in strips_at(s):
            c = last_of_chunk(k)
            if c is not None and not (last and g == GROUPS):
                at[min(s + 1, BODY)].append(("shift", g, c))
    n = 0
    for s in range(BODY):
        if ends_block(s):
            at[min(s + 2, BODY)].append(("out", n))
            n += 1
    if not last:
        s = 8
        for job in project_order():
            while at[s]:
                s += 1
            at[s].append(job)
            s += 1
    return at


def project_order():
    jobs = [("proj", 0)]
    for t in range(1, TILES):
        jobs += [("proj", t), ("turn", t - 1)]
    return jobs + [("turn", TILES - 1)]


def early_work():
    strips = list(range(len(EARLY_STRIPS)))
    work, shifts = [], []

    def strip():
        work.append(("strip", strips[0]))
        c = last_of_chunk(strips.pop(0))
        work.extend(shifts)
        shifts[:] = [] if c is None else [("shift", c)]

    for job in project_order():
        work.append(job)
        if job[0] == "turn" and job[1] >= FIRST_STRIP:
            for _ in range((job[1] - FIRST_STRIP) // TPC + 1):
                strip()
    while strips:
        strip()
    return work + shifts


def ring_distance(n):
    return RING if n >= A_ROUND % RING else A_ROUND % RING


def ends_block(s):
    c, kt, _ = STEPS[s % NS]
    return kt == TPC * (c + 1) - 1


def diagonal(s):
    c, kt, _ = STEPS[s % NS]
    return kt >= TPC * c


DIAG = [sum(diagonal(x) for x in range(s)) for s in range(BODY + 1)]
ENDS = [sum(ends_block(x) for x in range(s)) for s in range(BODY + 1)]
UNITS = [GH * sum(len(strips_at(x)) for x in range(s)) for s in range(BODY + 1)]
EARLY_UNITS = GH * len(EARLY_STRIPS)
A_ROUND = BODY * GH
assert A_ROUND == UNITS[BODY] and A_ROUND % RING > 0
EARLY = early_work()
EARLY_JOBS = sum(job != "strip" for job, _ in EARLY)
LOOP_JOBS, LAST_JOBS = round_jobs(False), round_jobs(True)
JOBS_A_ROUND = sum(map(len, LOOP_JOBS))
STACK_DMAS = len(SLOTS) * (1 + CHUNKS)
FIRST_STACK_DMAS = len(SLOTS) * 2
SHIFT_DMAS = SPLITS


def build(nc, x, wqkv, bqkv, wp, bp, cos, sin, ident_in, ffn, out, y_dram):
    x_tiles = x.rearrange("b (t p) c -> p (b t) c", p=P)
    out_tiles = out.rearrange("b (t p) c -> p (b t) c", p=P)
    NT = B * TILES
    with ExitStack() as ctx:
        def sem(name):
            return ctx.enter_context(nc.semaphore(name))

        def sb(scope, name, shape, dt=F32):
            return scope.enter_context(nc.sbuf_tensor(name, shape, dt))

        def pb(scope, name, shape):
            return scope.enter_context(nc.psum_tensor(name, shape, F32))

        xnT = sb(ctx, "xnT", [P, CT, B * T])
        ident = sb(ctx, "ident", [P, P])
        wp_sb = sb(ctx, "wp_sb", [P, CT, C])
        bp_sb = sb(ctx, "bp_sb", [P, CT])
        w1 = sb(ctx, "w1", [P, CT, C])
        b1 = sb(ctx, "b1", [P, CT])
        w2 = sb(ctx, "w2", [P, CT, P])
        b2 = sb(ctx, "b2", [P, 1])
        w3 = sb(ctx, "w3", [P, H3])
        b3 = sb(ctx, "b3", [P, 1])
        w4 = sb(ctx, "w4", [P, 1])
        w4_wide = sb(ctx, "w4_wide", [P, 2, P])
        b4 = sb(ctx, "b4", [P, 1])
        gw1 = sb(ctx, "gw1", [P, CT, P])
        gb1 = sb(ctx, "gb1", [P, 1])
        gw2 = sb(ctx, "gw2", [P, H3])
        gb2 = sb(ctx, "gb2", [H3, 1])
        gw3 = sb(ctx, "gw3", [H3, 1])
        gw3_wide = sb(ctx, "gw3_wide", [H3, P])
        gb3 = sb(ctx, "gb3", [P, 1])
        ar = sb(ctx, "ar", [P, 1])
        sign = sb(ctx, "sign", [P, 1])
        swing = sb(ctx, "swing", [P, 1])
        base = sb(ctx, "base", [P, B])
        xsum = sb(ctx, "xsum", [P, CT, B])
        gh1 = sb(ctx, "gh1", [P, B])
        gh2 = sb(ctx, "gh2", [H3, B])
        gtanh = sb(ctx, "gtanh", [P, B])

        stats = sb(ctx, "stats", [P, NT, 6])
        meanvar = sb(ctx, "meanvar", [P, NT, 2])
        std = sb(ctx, "std", [P, B, TILES])
        rstd = sb(ctx, "rstd", [P, B, TILES])

        with ExitStack() as s1:
            x_in = sb(s1, "x_in", [P, NT, C])
            ps_x = pb(s1, "ps_x", [P, 2, CT, QB])

        with ExitStack() as s2:
            qst = [sb(s2, f"qst{g}", [P, CHUNKS, GH, QB], BF16) for g in range(GROUPS)]
            kst = [sb(s2, f"kst{g}", [P, GH, T], BF16) for g in range(GROUPS)]
            parts = sb(s2, "parts", [P, 2, SPLITS, T], BF16)
            probs = sb(s2, "probs", [P, 2, GH, QB])
            vcur = [sb(s2, f"vcur{g}", [P, TILES, GH, VW]) for g in range(GROUPS)]
            vnext = sb(s2, "vnext", [P, GROUPS, TILES, GH, VW])
            xwin = sb(s2, "xwin", [P, 2, CT, QB])
            wcur = sb(s2, "wcur", [P, CT, QKV])
            bcur = sb(s2, "bcur", [P, QKV])
            cos_sb = sb(s2, "cos_sb", [P, TILES, HS])
            sin_sb = sb(s2, "sin_sb", [P, TILES, HS])
            qk_in = sb(s2, "qk_in", [P, 2, 2 * P])
            qk_cos = sb(s2, "qk_cos", [P, 2 * P])
            qk_rot = sb(s2, "qk_rot", [P, 2, 2 * P])
            rest = sb(s2, "rest", [P, 2, 2, P])
            mask = sb(s2, "mask", [P, QB])
            strip_max = sb(s2, "strip_max", [P, GH, TILES, CHUNKS])
            neg_max = sb(s2, "neg_max", [P, 2, GH, TPC])
            mparts = sb(s2, "mparts", [GH * TPC, 2, SPLITS, P], BF16)
            mrest = sb(s2, "mrest", [GH * TPC, P])
            o_sb = sb(s2, "o_sb", [P, 2, QB])
            recip = sb(s2, "recip", [P, TPC * GH])
            y_sb = sb(s2, "y_sb", [P, 2, TPC * GH * HS])
            ps_s = pb(s2, "ps_s", [P, RING, QB])
            ps_m = pb(s2, "ps_m", [P, RING, QB])
            ps_o = pb(s2, "ps_o", [P, QB])
            ps_j = pb(s2, "ps_j", [P, QB])

        with ExitStack() as s3:
            h1 = sb(s3, "h1", [P, 2, 2, CT, QB])
            h2 = sb(s3, "h2", [P, 2, 2, QB])
            h3 = sb(s3, "h3", [P, QB])
            th = sb(s3, "th", [P, 2, QB])
            coup = sb(s3, "coup", [P, 2, QB])
            prod = sb(s3, "prod", [P, 2, CT, QB])
            y_in = sb(s3, "y_in", [P, INPUTS, TPC, CT, P])
            x_res = sb(s3, "x_res", [P, INPUTS, TPC, C])
            yT = sb(s3, "yT", [P, RING, CT, P])
            res = sb(s3, "res", [P, 2, TPC, C])
            with ExitStack() as s4:
                ps_1 = pb(s4, "ps_1", [P, 2, QB])
                ps_2 = pb(s4, "ps_2", [P, 2, QB])
                ps_3 = pb(s4, "ps_3", [P, QB])
                ps_4 = pb(s4, "ps_4", [P, 2, QB])
                ps_g = pb(s4, "ps_g", [P, QB])
            with ExitStack() as s4:
                ps_t = pb(s4, "ps_t", [P, RING, QB])
                ps_y = pb(s4, "ps_y", [P, 2, QB])

        x_loaded = [sem(f"x_loaded{k}") for k in range(NT // TPC)]
        ident_loaded, weights_loaded, rope_loaded = sem("ident_loaded"), sem("weights_loaded"), sem("rope_loaded")
        stats_done, var_done, std_done, rstd_done = sem("stats_done"), sem("var_done"), sem("std_done"), sem("rstd_done")
        xn_ready, xt_ready, xt_copied = sem("xn_ready"), sem("xt_ready"), sem("xt_copied")
        set_up, pool_ones, zeros_set = sem("set_up"), sem("pool_ones"), sem("zeros_set")
        w_loaded = sem("w_loaded")
        win_loaded = [sem("win_loaded0"), sem("win_loaded1")]
        job_ready = sem("job_ready")
        v_ready, y_ready = sem("v_ready"), sem("y_ready")
        qk_ready, cos_done, rot_done = sem("qk_ready"), sem("cos_done"), sem("rot_done")
        hi_ready, rest_ready, mid_done, parts_ready = sem("hi_ready"), sem("rest_ready"), sem("mid_done"), sem("parts_ready")
        first_stack = [sem(f"first_stack{c}") for c in range(CHUNKS)]
        stack_loaded = [sem("stack_loaded0"), sem("stack_loaded1")]
        v_loaded = [sem("v_loaded0"), sem("v_loaded1")]
        max_ready, max_used = sem("max_ready"), sem("max_used")
        neg_ready, mhi_ready, mrest_ready, mmid_ready, mparts_ready = (sem(n) for n in (
            "neg_ready", "mhi_ready", "mrest_ready", "mmid_ready", "mparts_ready"))
        shift_loaded = [sem(f"shift_loaded{c}") for c in range(CHUNKS)]
        scores_ready, exp_done, mask_done, pv_done = sem("scores_ready"), sem("exp_done"), sem("mask_done"), sem("pv_done")
        o_copied, o_turned = sem("o_copied"), sem("o_turned")
        y_stored = [sem("y_stored0"), sem("y_stored1")]
        prep = sem("prep")
        l1_done, l2_done, l3_done, l4_done = sem("l1_done"), sem("l2_done"), sem("l3_done"), sem("l4_done")
        g1_done, g2_done, g3_done, th_done = sem("g1_done"), sem("g2_done"), sem("g3_done"), sem("th_done")
        coup_done, prod_done, upd_done = sem("coup_done"), sem("prod_done"), sem("upd_done")
        glob_mm, glob_act, glob_base = sem("glob_mm"), sem("glob_act"), sem("glob_base")
        yx_loaded = [sem(f"yx_loaded{k}") for k in range(INPUTS)]
        yt_ready, yt_copied, sum_ready, res_ready = sem("yt_ready"), sem("yt_copied"), sem("sum_ready"), sem("res_ready")
        out_stored = [sem("out_stored0"), sem("out_stored1")]

        def column(v):
            return v.rearrange("(p o) -> p o", o=1)

        weights = [
            (wp_sb[:], wp.rearrange("(c p) n -> p c n", p=P)), (bp_sb[:], bp),
            (w1[:], ffn["cn_w1"].rearrange("(c p) n -> p c n", p=P)), (b1[:], ffn["cn_b1"]),
            (w2[:], ffn["cn_w2"].rearrange("(c p) n -> p c n", p=P)), (b2[:], column(ffn["cn_b2"])),
            (w3[:], ffn["cn_w3"]), (b3[0:H3], column(ffn["cn_b3"])), (b3[H3:P], column(ffn["cn_b3"])),
            (w4[0:H3], ffn["cn_w4"]), (w4[H3:P], ffn["cn_w4"]),
            (b4[:], ffn["cn_b4"].partition_broadcast(P)),
            (gw1[:], ffn["gc_w1"].rearrange("(c p) n -> p c n", p=P)), (gb1[:], column(ffn["gc_b1"])),
            (gw2[:], ffn["gc_w2"]), (gb2[:], column(ffn["gc_b2"])),
            (gw3[:], ffn["gc_w3"]), (gb3[:], ffn["gc_b3"].partition_broadcast(P)),
            (ar[:], ffn["adaptive_range"].partition_broadcast(P)),
        ]
        PREP = 7

        def rounds(eng, body):
            with eng.Fori(0, NI - 1) as i:
                body(i, LOOP_JOBS, False)
            body(NI - 1, LAST_JOBS, True)

        def jobs_before(i, jobs, s):
            return EARLY_JOBS + i * JOBS_A_ROUND + sum(map(len, jobs[:s]))

        def unit_at(i, s):
            return (i + 1) * A_ROUND + (EARLY_UNITS - A_ROUND + UNITS[s])

        def spread(units):
            n, places = len(units), GH + 2
            cut = [n * k // places for k in range(places + 1)]
            return [units[a:b] for a, b in zip(cut, cut[1:])]

        DVE_AHEAD = 1

        def wait_alone(eng, semaphore, value):
            eng.wait_ge(semaphore, value)
            eng.nop(nofuse=True)

        block = ctx.enter_context(nc.Block())

        @block.sync
        def _(sp):
            for k in range(NT // TPC):
                sp.dma_start(x_in[:, k * TPC:(k + 1) * TPC, :],
                             x_tiles[:, k * TPC:(k + 1) * TPC, :]).then_inc(x_loaded[k], 16)
                if k == 0:
                    sp.dma_start(ident[:], ident_in).then_inc(ident_loaded, 16)
            def load_weights(r):
                sp.dma_start(wcur[:], wqkv[bass.ds(r, 1), :, :].rearrange("i (c p) n -> p (i c) n", p=P)
                             ).then_inc(w_loaded, 16)
                sp.dma_start(bcur[:], bqkv[bass.ds(r, 1), :, :].rearrange("i p n -> (i p) n")).then_inc(w_loaded, 16)

            load_weights(0)
            sp.dma_start(cos_sb[:], cos).then_inc(rope_loaded, 16)
            sp.dma_start(sin_sb[:], sin).then_inc(rope_loaded, 16)
            for dst, src in weights:
                sp.dma_start(dst, src).then_inc(weights_loaded, 16)

            def load_window(r, cc):
                sp.dma_start(xwin[:, cc % 2], xnT[:, :, bass.ds((r // CT) * T + cc * QB, QB)]
                             ).then_inc(win_loaded[cc % 2], 16)

            def load_stack(g):
                for n, (_, kpart) in enumerate(SLOTS):
                    sp.dma_start(kst[g][HS * n:HS * (n + 1)],
                                 parts[heads(g), 1, kpart, :]).then_inc(stack_loaded[g], 16)
                for c in range(CHUNKS):
                    load_stack_q(g, c, stack_loaded[g])

            def heads(g):
                return slice(HS * GH * g, HS * GH * (g + 1))

            def load_stack_q(g, c, done):
                for n, (qpart, _) in enumerate(SLOTS):
                    sp.dma_start(qst[g][HS * n:HS * (n + 1), c],
                                 parts[heads(g), 0, qpart, c * QB:(c + 1) * QB]).then_inc(done, 16)

            def load_first_stack(c):
                for n, (_, kpart) in enumerate(SLOTS):
                    sp.dma_start(kst[0][HS * n:HS * (n + 1), :, c * QB:(c + 1) * QB],
                                 parts[heads(0), 1, kpart, c * QB:(c + 1) * QB]).then_inc(first_stack[c], 16)
                load_stack_q(0, c, first_stack[c])

            def load_v(g):
                sp.dma_start(vcur[g][:].rearrange("p t h d -> p (t h d)"),
                             vnext[:, g].rearrange("p t h d -> p (t h d)")).then_inc(v_loaded[g], 16)

            def load_shift(g, c):
                for p in range(SPLITS):
                    sp.dma_start(qst[g % GROUPS][SHIFT + p:SHIFT + p + 1, c],
                                 mparts[:, c % 2, p, :]).then_inc(shift_loaded[c], 16)

            for cc in (0, 1):
                sp.wait_ge(xt_copied, CT * (cc + 1))
                load_window(0, cc)
            for job, t in EARLY:
                c = t // TPC
                if job == "proj" and t in (TPC - 1, 2 * TPC - 1):
                    sp.wait_ge(qk_ready, TPC * (c + 1))
                    sp.wait_ge(xt_copied, CT * (c + 3))
                    load_window(0, c + 2)
                elif job == "turn" and t % TPC == TPC - 1:
                    sp.wait_ge(parts_ready, TPC * (c + 1))
                    if c == 0:
                        sp.wait_ge(xt_ready, CT * NT // TPC)
                    load_first_stack(c)
                elif job == "shift":
                    sp.wait_ge(mparts_ready, t + 1)
                    load_shift(0, t)
            sp.wait_ge(v_ready, TILES)
            load_v(0)

            def store(k):
                sp.wait_ge(res_ready, TPC * (k + 1))
                sp.dma_start(out_tiles[:, k * TPC:(k + 1) * TPC, :], res[:, k % 2]).then_inc(out_stored[k % 2], 16)

            def body(i, jobs, last):
                if not last:
                    sp.wait_ge(v_ready, (i + 1) * TILES)
                    load_weights(i + 1)
                    for cc in (0, 1):
                        load_window(i + 1, cc)
                sp.wait_ge(scores_ready, i * A_ROUND + GH)
                load_stack(1)
                pending = []
                for s in range(BODY + 1):
                    if s == 1:
                        sp.wait_ge(pv_done, i * BODY + 1)
                        load_v(1)
                    for job in pending:
                        if job[0] == "shift":
                            sp.wait_ge(mparts_ready, i * GROUPS * CHUNKS + CHUNKS * job[1] + job[2] + 1)
                            load_shift(job[1], job[2])
                        elif job[0] == "out":
                            store_y(i, job[1])
                        elif job[0] == "proj" and job[1] in (TPC - 1, 2 * TPC - 1):
                            cc = job[1] // TPC + 2
                            sp.wait_ge(qk_ready, (i + 1) * TILES + TPC * (cc - 1))
                            load_window(i + 1, cc)
                        elif job == ("turn", TILES - 1):
                            sp.wait_ge(scores_ready, i * A_ROUND + GH * NS)
                            sp.wait_ge(parts_ready, (i + 2) * TILES)
                            load_stack(0)
                            sp.wait_ge(pv_done, i * BODY + NS)
                            load_v(0)
                    pending = jobs[s]
                for job in pending:
                    store_y(i, job[1])

            def store_y(i, n):
                sp.wait_ge(y_ready, i * ENDS[BODY] + n + 2)
                g, c = divmod(n, CHUNKS)
                sp.dma_start(
                    y_dram[bass.ds(i, 1), c * QB:(c + 1) * QB, g * GH * HS:(g + 1) * GH * HS]
                    .rearrange("i (t p) d -> p (i t) d", p=P),
                    y_sb[:, n % 2].rearrange("p (t d) -> p t d", t=TPC)).then_inc(y_stored[n % 2], 16)

            rounds(sp, body)

            for p in range(2):
                sp.wait_ge(y_stored[p], NI * ENDS[BODY] // 2 * 16 + 1)
            sp.wait_ge(pv_done, NI * BODY)
            def load(k):
                b, c = divmod(k, CHUNKS)
                at = k % INPUTS
                for half in range(CT):
                    sp.dma_start(y_in[:, at, :, half, :], y_dram[CT * b + half, c * QB:(c + 1) * QB, :]
                                 .rearrange("(t p) d -> p t d", p=P)).then_inc(yx_loaded[at], 16)
                sp.dma_start(x_res[:, at], x_tiles[:, k * TPC:(k + 1) * TPC, :]).then_inc(yx_loaded[at], 16)

            for k in range(INPUTS):
                load(k)
            for k in range(NT // TPC):
                store(k)
                if k + INPUTS < NT // TPC:
                    load(k + INPUTS)
            for p in range(2):
                sp.wait_ge(out_stored[p], NT // TPC // 2 * 16)

        @block.gpsimd
        def _(pool):
            nc.gpsimd.memset(mask[:], 0.0).then_inc(set_up, 1)
            pool.wait_ge(set_up, 1)
            nc.gpsimd.affine_select(out=mask[:, QB - P:], in_=mask[:, QB - P:], pattern=[[-1, P]],
                                    compare_op=ALU.is_ge, fill=NEG, base=0,
                                    channel_multiplier=1).then_inc(set_up, 1)
            nc.gpsimd.memset(vnext[:], 1.0).then_inc(pool_ones, 1)
            for g in range(GROUPS):
                pool.wait_ge(pool_ones, g + 1)
                nc.gpsimd.memset(kst[g][SHIFT:KROWS], 1.0).then_inc(pool_ones, 1)
            pool.wait_ge(rope_loaded, 32)

            def rotate(r, t):
                n = r * TILES + t
                src, dst, cosines = (a.rearrange("p (g d h) -> p g d h", d=HS, h=GH) for a in (
                    qk_in[:, t % 2], qk_rot[:, t % 2], qk_cos[:]))

                def table(tab, a, step):
                    return tab[:, t:t + 1, a::step].rearrange("p g (d h) -> p g d h", h=1).broadcast_to(
                        [P, 2 * GROUPS, HS // step, GH])

                if not (isinstance(n, int) and n == 0):
                    pool.wait_ge(rot_done, n)
                pool.wait_ge(qk_ready, n + 1)
                nc.gpsimd.tensor_tensor(cosines, src,
                                        table(cos_sb, 0, 1), ALU.mult).then_inc(cos_done, 1)
                if not (isinstance(r, int) and r == 0 and t < 2):
                    pool.wait_ge(rest_ready, n - 1)
                for a in (0, 1):
                    nc.gpsimd.tensor_tensor(dst[:, :, a::2, :], src[:, :, 1 - a::2, :],
                                            table(sin_sb, a, 2), ALU.mult).then_inc(cos_done, 1)
                pool.wait_ge(cos_done, 3 * (n + 1))
                nc.gpsimd.tensor_tensor(qk_rot[:, t % 2], qk_rot[:, t % 2], qk_cos[:],
                                        ALU.add).then_inc(rot_done, 1)

            def split(r, t):
                n = r * TILES + t
                at = slice(t * P, (t + 1) * P)
                if not (isinstance(r, int) and r == 0):
                    wait_alone(pool, rest_ready, n + 1)
                    nc.gpsimd.tensor_copy(parts[:, :, 1, at], rest[:, t % 2]).then_inc(mid_done, 1)
                pool.wait_ge(mid_done, n + 1)
                nc.gpsimd.tensor_tensor(parts[:, :, 2, at], rest[:, t % 2], parts[:, :, 1, at],
                                        ALU.subtract).then_inc(parts_ready, 1)

            def mask_step(i, s):
                lo = STEPS[s % NS][2]
                wait_alone(pool, exp_done, i * A_ROUND + GH * (s + 1))
                blockp = probs[:, s % 2, :, lo:lo + P]
                nc.gpsimd.affine_select(out=blockp, in_=blockp, pattern=[[0, GH], [1, P]],
                                        compare_op=ALU.is_ge, fill=0.0, base=0,
                                        channel_multiplier=-1).then_inc(mask_done, 1)

            for job, t in project_order():
                rotate(0, t) if job == "proj" else split(0, t)
            mask_step(0, 0)

            def body(i, jobs, last):
                for s in range(BODY):
                    if s + 1 < BODY:
                        if diagonal(s + 1):
                            mask_step(i, s + 1)
                    elif not last:
                        mask_step(i + 1, 0)
                    for job in jobs[s]:
                        if job[0] == "proj":
                            rotate(i + 1, job[1])
                        elif job[0] == "turn":
                            split(i + 1, job[1])

            rounds(pool, body)

        @block.scalar
        def _(act):
            for b in range(B):
                act.wait_ge(var_done, b + 1)
                nc.scalar.activation(std[:, b, :], std[:, b, :], ACT.Sqrt).then_inc(std_done, 1)
            for k in range(NT // TPC):
                for c in range(CT):
                    act.wait_ge(xt_ready, k * CT + c + 1)
                    nc.scalar.activation(xnT[:, c, k * QB:(k + 1) * QB], ps_x[:, k % 2, c, :],
                                         ACT.Copy).then_inc(xt_copied, 1)

            def exps(i, s):
                lo = STEPS[s % NS][2]
                for h in range(GH):
                    n = GH * s + h
                    act.wait_ge(scores_ready, i * A_ROUND + n + 1)
                    if h == 0 and s >= 2:
                        act.wait_ge(pv_done, i * BODY + s - 1)
                    elif h == 0 and s == 0 and not (isinstance(i, int) and i == 0):
                        act.wait_ge(pv_done, i * BODY - 1)
                    nc.scalar.activation(probs[:, s % 2, h, lo:], ps_s[:, n % RING, lo:], ACT.Exp,
                                         scale=SCALE).then_inc(exp_done, 1)

            def high(r, t, number):
                act.wait_ge(job_ready, number + 1)
                if t == 0 and not (isinstance(r, int) and r == 0):
                    act.wait_ge(stack_loaded[1], r * STACK_DMAS * 16)
                nc.scalar.activation(parts[:, :, 0, t * P:(t + 1) * P],
                                     ps_j[:, 0:2 * P].rearrange("p (a n) -> p a n", a=2),
                                     ACT.Copy).then_inc(hi_ready, 1)

            def shift_high(g, c, number):
                act.wait_ge(job_ready, number + 1)
                if c >= 2:
                    act.wait_ge(shift_loaded[c - 2], (g + 1) * SHIFT_DMAS * 16)
                elif not (isinstance(g, int) and g == 0):
                    act.wait_ge(shift_loaded[c + 2], g * SHIFT_DMAS * 16)
                nc.scalar.activation(mparts[:, c % 2, 0, :], ps_j[0:GH * TPC, 0:P],
                                     ACT.Copy).then_inc(mhi_ready, 1)

            def copy_out(i, s):
                n = ENDS[s]
                act.wait_ge(pv_done, i * BODY + s + 1)
                act.wait_ge(o_turned, i * ENDS[BODY] + max(n - 1, 0) + 1)
                nc.scalar.activation(o_sb[:, n % 2], ps_o[:], ACT.Copy).then_inc(o_copied, 1)

            number = 0
            for job, t in EARLY:
                if job == "turn":
                    high(0, t, number)
                    act.wait_ge(rest_ready, t + 1)
                    nc.scalar.activation(parts[:, :, 1, t * P:(t + 1) * P], rest[:, t % 2],
                                         ACT.Copy).then_inc(mid_done, 1)
                elif job == "shift":
                    shift_high(0, t, number)
                number += job != "strip"
            exps(0, 0)

            def body(i, jobs, last):
                for s in range(BODY + 1):
                    if s + 1 < BODY:
                        exps(i, s + 1)
                    elif s + 1 == BODY and not last:
                        exps(i + 1, 0)
                    for n, job in enumerate(jobs[s]):
                        number = jobs_before(i, jobs, s) + n
                        if job[0] == "turn":
                            high(i + 1, job[1], number)
                        elif job[0] == "shift":
                            shift_high(i * GROUPS + job[1], job[2], number)
                    if s < BODY and ends_block(s):
                        copy_out(i, s)

            rounds(act, body)

            for p in range(2):
                act.wait_ge(y_stored[p], NI * ENDS[BODY] // 2 * 16 + 1)

            def gelu(out_, in_, bias, done):
                nc.scalar.activation(out_, in_, ACT.Gelu, bias=bias).then_inc(done, 1)

            def gelu_1(n, blk):
                for m in range(CT):
                    u = 4 * n + CT * blk + m
                    act.wait_ge(l1_done, u + 1)
                    if n >= 2:
                        act.wait_ge(l2_done, 2 * (n - 2) + blk + 1)
                    gelu(h1[:, n % 2, blk, m, :], ps_1[:, m, :], b1[:, m:m + 1], g1_done)

            def global_net(stage):
                act.wait_ge(glob_mm, stage + 1)
                if stage == 0:
                    gelu(gh1[:], ps_g[:, 0:B], gb1[:, 0:1], glob_act)
                elif stage == 1:
                    gelu(gh2[:], ps_g[0:H3, 0:B], gb2[:, 0:1], glob_act)
                else:
                    nc.scalar.activation(gtanh[:], ps_g[:, 0:B], ACT.Tanh, bias=gb3[:, 0:1],
                                         scale=0.5).then_inc(glob_act, 1)

            act.wait_ge(weights_loaded, 16 * len(weights))
            act.wait_ge(prep, PREP)
            for n in range(CYCLES * PAIRS + 2):
                if n < CYCLES * PAIRS:
                    gelu_1(n, 0)
                if n >= 2:
                    m = n - 2
                    act.wait_ge(l3_done, m + 1)
                    if m >= 1:
                        act.wait_ge(l4_done, 2 * m)
                    gelu(h3[:], ps_3[:], b3[:, 0:1], g3_done)
                if n < CYCLES * PAIRS:
                    gelu_1(n, 1)
                if n >= 2:
                    for blk in range(2):
                        act.wait_ge(l4_done, 2 * m + blk + 1)
                        if m >= 1:
                            act.wait_ge(coup_done, 2 * (m - 1) + blk + 1)
                        nc.scalar.activation(th[:, blk, :], ps_4[:, blk, :], ACT.Tanh, bias=b4[:, 0:1],
                                             scale=0.5).then_inc(th_done, 1)
                if n < 3:
                    global_net(n)
                if 1 <= n <= CYCLES * PAIRS:
                    m = n - 1
                    for blk in range(2):
                        act.wait_ge(l2_done, 2 * m + blk + 1)
                        if m >= 2:
                            act.wait_ge(l3_done, m - 1)
                        gelu(h2[:, m % 2, blk, :], ps_2[:, blk, :], b2[:, 0:1], g2_done)

            for t in range(NT):
                act.wait_ge(yt_ready, t + 1)
                if t >= RING:
                    act.wait_ge(sum_ready, t - RING + 1)
                nc.scalar.activation(yT[:, t % RING], ps_t[:, t % RING, 0:C].rearrange("p (c n) -> p c n", c=CT),
                                     ACT.Copy).then_inc(yt_copied, 1)

        @block.vector
        def _(dve):
            for b in range(B):
                tiles = range(b * TILES, (b + 1) * TILES)
                for t in tiles:
                    if t % TPC == 0:
                        dve.wait_ge(x_loaded[t // TPC], 16)
                    nc.vector.bn_stats(stats[:, t, :], x_in[:, t, :]).then_inc(stats_done, 1)
                for n, t in enumerate(tiles):
                    dve.wait_ge(stats_done, 2 * TILES * b + n + 1)
                    nc.vector.bn_aggr(meanvar[:, t, :], stats[:, t, :]).then_inc(stats_done, 1)
                dve.wait_ge(stats_done, 2 * TILES * (b + 1))
                nc.vector.tensor_scalar(std[:, b, :], meanvar[:, b * TILES:(b + 1) * TILES, 1], EPS, None,
                                        ALU.add).then_inc(var_done, 1)
                dve.wait_ge(std_done, b + 1)
                nc.vector.reciprocal(rstd[:, b, :], std[:, b, :]).then_inc(rstd_done, 1)
                dve.wait_ge(rstd_done, b + 1)
                for n, t in enumerate(tiles):
                    nc.vector.tensor_scalar(x_in[:, t, :], x_in[:, t, :], meanvar[:, t, 0:1],
                                            rstd[:, b, n:n + 1], ALU.subtract, ALU.mult).then_inc(xn_ready, 1)

            dve.wait_ge(weights_loaded, 16 * len(weights))
            nc.vector.memset(sign[0:H3], 1.0).then_inc(prep, 1)
            nc.vector.memset(sign[H3:P], -1.0).then_inc(prep, 1)
            nc.vector.memset(w4_wide[:], 0.0).then_inc(prep, 1)
            dve.wait_ge(prep, 3)
            nc.vector.tensor_scalar(b4[:], b4[:], 0.5, None, ALU.mult).then_inc(prep, 1)
            nc.vector.tensor_scalar(gb3[:], gb3[:], 0.5, None, ALU.mult).then_inc(prep, 1)
            for blk in range(2):
                rows = slice(H3 * blk, H3 * (blk + 1))
                nc.vector.tensor_scalar(w4_wide[rows, blk, :], w4_wide[rows, blk, :], w4[rows, 0:1], None,
                                        ALU.add).then_inc(prep, 1)
            nc.vector.tensor_scalar(swing[:], ar[:], sign[:, 0:1], 0.3, ALU.mult, ALU.mult).then_inc(glob_base, 1)
            nc.vector.memset(gw3_wide[:], 0.0).then_inc(glob_base, 1)
            dve.wait_ge(glob_base, 2)
            nc.vector.tensor_scalar(gw3_wide[:], gw3_wide[:], gw3[:, 0:1], None, ALU.add).then_inc(glob_base, 1)

            nc.vector.memset(ps_o[:], 0.0).then_inc(zeros_set, 1)
            dve.wait_ge(pool_ones, 3)
            dve.wait_ge(zeros_set, 1)
            for free, buf in ((o_turned, o_sb[:, 0, 0:1]), (y_ready, recip[:, 0:1]),
                              (y_stored[0], y_sb[:, 0, 0:1]), (y_stored[1], y_sb[:, 1, 0:1])):
                nc.vector.memset(buf, 0.0).then_inc(free, 1)

            def project(r, t, number):
                n = r * TILES + t
                first = isinstance(r, int) and r == 0
                dve.wait_ge(job_ready, number + 1)
                if not (first and t < 2):
                    dve.wait_ge(rot_done, n - 1)
                nc.vector.tensor_tensor(qk_in[:, t % 2], ps_j[:, 0:2 * P], bcur[:, 0:2 * P],
                                        ALU.add).then_inc(qk_ready, 1)
                if t == 0 and not first:
                    for g in range(GROUPS):
                        dve.wait_ge(v_loaded[g], r * 16)
                nc.vector.tensor_tensor(vnext[:, :, t, :, 0:HS],
                                        ps_j[:, 2 * P:3 * P].rearrange("p (g h d) -> p g h d", g=GROUPS, h=GH),
                                        bcur[:, 2 * P:3 * P].rearrange("p (g h d) -> p g h d", g=GROUPS, h=GH),
                                        ALU.add).then_inc(v_ready, 1)

            def remainder(r, t):
                n = r * TILES + t
                dve.wait_ge(hi_ready, n + 1)
                if not (isinstance(r, int) and r == 0 and t < 2):
                    dve.wait_ge(parts_ready, n - 1)
                nc.vector.tensor_tensor(rest[:, t % 2], ps_j[:, 0:2 * P].rearrange("p (a n) -> p a n", a=2),
                                        parts[:, :, 0, t * P:(t + 1) * P], ALU.subtract).then_inc(rest_ready, 1)

            def strip(g, k, h, unit, place):
                t, kb, w = STRIPS[k]
                at = strip_max[:, h, t, kb:kb + 1]
                scores = ps_m[:, place % RING, 0:w]
                if kb == t // TPC:
                    dve.wait_ge(set_up, 2)
                    wait_alone(dve, max_ready, unit + 1)
                else:
                    dve.wait_ge(max_ready, unit + 1)
                if kb == t // TPC:
                    nc.vector.tensor_tensor_reduce(scores, scores, mask[:, QB - w:], 1.0, NEG,
                                                   ALU.add, ALU.max, at).then_inc(max_used, 1)
                else:
                    nc.vector.tensor_reduce(at, scores, AX_X, ALU.max).then_inc(max_used, 1)

            def chunk_max(c, units):
                dve.wait_ge(max_used, units)
                nc.vector.tensor_reduce(neg_max[:, c % 2], strip_max[:, :, TPC * c:TPC * (c + 1), 0:c + 1],
                                        AX_X, ALU.max, negate=True).then_inc(neg_ready, 1)

            def shift(c, n):
                m = mparts[:, c % 2]
                dve.wait_ge(mhi_ready, n + 1)
                nc.vector.tensor_tensor(mrest[:], ps_j[0:GH * TPC, 0:P], m[:, 0, :],
                                        ALU.subtract).then_inc(mrest_ready, 1)
                dve.wait_ge(mrest_ready, n + 1)
                nc.vector.tensor_copy(m[:, 1, :], mrest[:]).then_inc(mmid_ready, 1)
                dve.wait_ge(mmid_ready, n + 1)
                nc.vector.tensor_tensor(m[:, 2, :], mrest[:], m[:, 1, :], ALU.subtract).then_inc(mparts_ready, 1)

            def normalise(i, n, number):
                turned = ps_j[:].rearrange("p (a d) -> p a d", d=2 * HS)
                dve.wait_ge(job_ready, number + 1)
                nc.vector.reciprocal(recip[:].rearrange("p (a d) -> p a d", d=1),
                                     turned[:, :, HS:VW]).then_inc(o_turned, 1)
                dve.wait_ge(o_turned, i * ENDS[BODY] + n + 2)
                dve.wait_ge(y_stored[n % 2], (i * (ENDS[BODY] // 2) + n // 2) * 16 + 1)
                nc.vector.tensor_tensor(y_sb[:, n % 2].rearrange("p (a d) -> p a d", d=HS), turned[:, :, 0:HS],
                                        recip[:].rearrange("p (a d) -> p a d", d=1)
                                        .broadcast_to([P, TPC * GH, HS]), ALU.mult).then_inc(y_ready, 1)

            unit = number = 0
            for job, t in EARLY:
                if job == "proj":
                    project(0, t, number)
                elif job == "turn":
                    remainder(0, t)
                elif job == "shift":
                    shift(t, t)
                else:
                    for h in range(GH):
                        strip(0, t, h, unit, A_ROUND - EARLY_UNITS + unit)
                        unit += 1
                    if last_of_chunk(t) is not None:
                        chunk_max(last_of_chunk(t), unit)
                number += job != "strip"

            def read_jobs(i, jobs, s):
                for n, job in enumerate(jobs[s] if s >= 0 else []):
                    number = jobs_before(i, jobs, s) + n
                    if job[0] == "proj":
                        project(i + 1, job[1], number)
                    elif job[0] == "turn":
                        remainder(i + 1, job[1])
                    elif job[0] == "shift":
                        shift(job[2], (i * GROUPS + job[1]) * CHUNKS + job[2])
                    else:
                        normalise(i, job[1], number)

            def body(i, jobs, last):
                for s in range(BODY + 1):
                    units = [(g, k, h) for g, k in (strips_at(s) if s < BODY else [])
                             if not (last and g == GROUPS) for h in range(GH)]
                    for n, (g, k, h) in enumerate(units):
                        if n == DVE_AHEAD:
                            read_jobs(i, jobs, s - 1)
                        strip(g, k, h, unit_at(i, s) + n, UNITS[s] + n)
                        c = last_of_chunk(k)
                        if c is not None and h == GH - 1:
                            chunk_max(c, unit_at(i, s) + n + 1)
                    if len(units) <= DVE_AHEAD:
                        read_jobs(i, jobs, s - 1)
                read_jobs(i, jobs, BODY)

            rounds(dve, body)

            for p in range(2):
                dve.wait_ge(y_stored[p], NI * ENDS[BODY] // 2 * 16 + 1)
            for c in range(CT):
                nc.vector.tensor_reduce(xsum[:, c, :], xnT[:, c, :].rearrange("p (b t) -> p b t", b=B), AX_X,
                                        ALU.add).then_inc(glob_base, 1)
            dve.wait_ge(glob_base, 3 + CT)
            nc.vector.tensor_scalar(xsum[:], xsum[:], 1.0 / T, None, ALU.mult).then_inc(glob_base, 1)
            dve.wait_ge(glob_act, 3)
            nc.vector.tensor_scalar(base[:], gtanh[:], ar[:, 0:1], 0.7, ALU.mult, ALU.mult).then_inc(glob_base, 1)
            dve.wait_ge(glob_base, 5 + CT)
            nc.vector.tensor_scalar(base[:], base[:], 0.1, sign[:, 0:1], ALU.add, ALU.mult).then_inc(glob_base, 1)
            dve.wait_ge(glob_base, 6 + CT)

            for m in range(CYCLES * PAIRS):
                for blk in range(2):
                    n = 2 * m + blk
                    p = m % PAIRS
                    b = p * B // PAIRS
                    tok = slice((2 * p + blk) * QB, (2 * p + blk + 1) * QB)
                    dve.wait_ge(th_done, n + 1)
                    nc.vector.tensor_scalar(coup[:, blk, :], th[:, blk, :], swing[:, 0:1], base[:, b:b + 1],
                                            ALU.mult, ALU.add).then_inc(coup_done, 1)
                    dve.wait_ge(coup_done, n + 1)
                    for c in range(CT):
                        nc.vector.tensor_tensor(prod[:, blk, c, :], coup[:, blk, :], xnT[:, 1 - c, tok],
                                                ALU.mult).then_inc(prod_done, 1)
                    dve.wait_ge(prod_done, 2 * n + 2)
                    for c, op in ((0, ALU.add), (1, ALU.subtract)):
                        if m < (CYCLES - 1) * PAIRS:
                            nc.vector.tensor_tensor(xnT[:, c, tok], xnT[:, c, tok], prod[:, blk, c, :],
                                                    op).then_inc(upd_done, 1)
                        else:
                            nc.vector.scalar_tensor_tensor(xnT[:, c, tok], xnT[:, c, tok], bp_sb[:, c:c + 1],
                                                           prod[:, blk, c, :], ALU.add, op).then_inc(upd_done, 1)

            for t in range(NT):
                k = t // TPC
                dve.wait_ge(sum_ready, t + 1)
                dve.wait_ge(yx_loaded[k % INPUTS], (k // INPUTS + 1) * 48)
                if t % TPC == 0 and k >= 2:
                    dve.wait_ge(out_stored[k % 2], (k // 2) * 16)
                nc.vector.tensor_tensor(res[:, k % 2, t % TPC, :], ps_y[:, t % 2, 0:C], x_res[:, k % INPUTS, t % TPC, :],
                                        ALU.add).then_inc(res_ready, 1)

        @block.tensor
        def _(pe):
            pe.wait_ge(ident_loaded, 16)
            for k in range(NT // TPC):
                if k >= 2:
                    pe.wait_ge(xt_copied, CT * (k - 1))
                pe.wait_ge(xn_ready, TPC * (k + 1))
                for c in range(CT):
                    for t in range(TPC):
                        last = nc.tensor.transpose(ps_x[:, k % 2, c, t * P:(t + 1) * P],
                                                   x_in[:, k * TPC + t, c * P:(c + 1) * P], ident[:])
                    last.then_inc(xt_ready, 1)

            def bank_free(r, i, job):
                if job[0] == "proj":
                    pe.wait_ge(v_ready, r * TILES + job[1] + 1)
                elif job[0] == "turn":
                    pe.wait_ge(rest_ready, r * TILES + job[1] + 1)
                elif job[0] == "shift":
                    pe.wait_ge(mrest_ready, (i * GROUPS + job[1]) * CHUNKS + job[2] + 1)
                else:
                    pe.wait_ge(y_ready, i * ENDS[BODY] + job[1] + 2)

            def project(r, t):
                if t == 0:
                    pe.wait_ge(w_loaded, (r + 1) * 32)
                cc = t // TPC
                if t % TPC == 0:
                    pe.wait_ge(win_loaded[cc % 2], (r * 2 + cc // 2 + 1) * 16)
                at = slice(t % TPC * P, (t % TPC + 1) * P)
                for c in range(CT):
                    last = nc.tensor.matmul(ps_j[:, 0:QKV], xwin[:, cc % 2, c, at], wcur[:, c, :],
                                            start=(c == 0), stop=(c == CT - 1))
                last.then_inc(job_ready, 1)

            def turn(r, t):
                pe.wait_ge(rot_done, r * TILES + t + 1)
                for side in range(2):
                    last = nc.tensor.transpose(ps_j[:, side * P:(side + 1) * P],
                                               qk_rot[:, t % 2, side * P:(side + 1) * P], ident[:])
                last.then_inc(job_ready, 1)

            def turn_max(n, c):
                pe.wait_ge(neg_ready, n + 1)
                nc.tensor.transpose(ps_j[0:GH * TPC, 0:P], neg_max[:, c % 2].rearrange("p h t -> p (h t)"),
                                    ident[:]).then_inc(job_ready, 1)

            def turn_out(i, n):
                pe.wait_ge(o_copied, i * ENDS[BODY] + n + 1)
                for t in range(TPC):
                    last = nc.tensor.transpose(ps_j[:, t * P:(t + 1) * P], o_sb[:, n % 2, t * P:(t + 1) * P],
                                               ident[:])
                last.then_inc(job_ready, 1)

            def strip(g, k, h, unit, place):
                t, kb, w = STRIPS[k]
                buf = g % GROUPS
                if not (isinstance(unit, int) and unit < RING):
                    pe.wait_ge(max_used, unit + 1 - ring_distance(place))
                nc.tensor.matmul(ps_m[:, place % RING, 0:w], qst[buf][0:ROWS, t // TPC, h, t % TPC * P:(t % TPC + 1) * P],
                                 kst[buf][0:ROWS, h, kb * QB:kb * QB + w], start=True, stop=True
                                 ).then_inc(max_ready, 1)

            def scores(i, s, h):
                g, n = divmod(s, NS)
                c, kt, lo = STEPS[n]
                if h == 0 and kt == 0:
                    pe.wait_ge(shift_loaded[c], (i * GROUPS + g + 1) * SHIFT_DMAS * 16)
                n = GH * s + h
                if not (isinstance(i, int) and i * A_ROUND + n < RING):
                    pe.wait_ge(exp_done, i * A_ROUND + n + 1 - ring_distance(n))
                nc.tensor.matmul(ps_s[:, n % RING, lo:], kst[g][0:KROWS, h, kt * P:(kt + 1) * P],
                                 qst[g][0:KROWS, c, h, lo:], start=True, stop=True
                                 ).then_inc(scores_ready, 1)

            def values(i, s):
                g, n = divmod(s, NS)
                c, kt, lo = STEPS[n]
                if diagonal(s):
                    pe.wait_ge(mask_done, i * DIAG[BODY] + DIAG[s] + 1)
                else:
                    pe.wait_ge(exp_done, i * A_ROUND + GH * (s + 1))
                if n == 0:
                    pe.wait_ge(v_loaded[g], (i + 1) * 16)
                if kt == 0 and s > 0:
                    pe.wait_ge(o_copied, i * ENDS[BODY] + ENDS[s])
                for h in range(GH):
                    last = nc.tensor.matmul(ps_o[2 * HS * h:2 * HS * h + VW, lo:], vcur[g][:, kt, h, :],
                                            probs[:, s % 2, h, lo:], start=(kt == 0),
                                            stop=(kt == TPC * (c + 1) - 1))
                last.then_inc(pv_done, 1)

            pe.wait_ge(xt_copied, CT * NT // TPC)
            pe.wait_ge(pool_ones, 3)
            pe.wait_ge(zeros_set, 1)
            before = None
            unit = 0
            for job, t in EARLY:
                if job == "strip":
                    if t == 0 or last_of_chunk(t - 1) is not None:
                        pe.wait_ge(first_stack[STRIPS[t][0] // TPC], FIRST_STACK_DMAS * 16)
                    for h in range(GH):
                        strip(0, t, h, unit, A_ROUND - EARLY_UNITS + unit)
                        unit += 1
                    continue
                if before:
                    bank_free(0, 0, before)
                if job == "proj":
                    project(0, t)
                elif job == "turn":
                    turn(0, t)
                else:
                    turn_max(t, t)
                before = (job, 0, t) if job == "shift" else (job, t)
            pe.wait_ge(first_stack[CHUNKS - 1], FIRST_STACK_DMAS * 16)
            for h in range(GH):
                scores(0, 0, h)
            early = len([k for _, k in EARLY_STRIPS if last_of_chunk(k) is not None])

            def body(i, jobs, last):
                before = None
                for s in range(BODY + 1):
                    strips = [(g, k) for g, k in (strips_at(s) if s < BODY else []) if not (last and g == GROUPS)]
                    units = [(g, k, h) for g, k in strips for h in range(GH)]
                    for g, k in strips:
                        if k == 0:
                            pe.wait_ge(stack_loaded[g % GROUPS], (i + 1) * STACK_DMAS * 16)
                    number = 0
                    for place, few in enumerate(spread(units)):
                        for g, k, h in few:
                            strip(g, k, h, unit_at(i, s) + number, UNITS[s] + number)
                            number += 1
                        if place < GH and s + 1 < BODY:
                            scores(i, s + 1, place)
                        elif place < GH and s + 1 == BODY and not last:
                            scores(i + 1, 0, place)
                        elif place == GH and s < BODY:
                            values(i, s)
                    for job in jobs[s]:
                        if before:
                            bank_free(i + 1, i, before)
                        else:
                            pe.wait_ge(v_ready, (i + 1) * TILES)
                            pe.wait_ge(rest_ready, (i + 1) * TILES)
                            pe.wait_ge(mrest_ready, i * GROUPS * CHUNKS + early)
                            pe.wait_ge(y_ready, i * ENDS[BODY] + 1)
                        if job[0] == "proj":
                            project(i + 1, job[1])
                        elif job[0] == "turn":
                            turn(i + 1, job[1])
                        elif job[0] == "shift":
                            turn_max((i * GROUPS + job[1]) * CHUNKS + job[2], job[2])
                        else:
                            turn_out(i, job[1])
                        before = job

            rounds(pe, body)

            def layer_1(n, blk):
                p = n % PAIRS
                tok = slice((2 * p + blk) * QB, (2 * p + blk + 1) * QB)
                if n >= PAIRS:
                    pe.wait_ge(upd_done, 2 * (2 * (n - PAIRS) + blk + 1))
                for m in range(CT):
                    u = 4 * n + CT * blk + m
                    if u >= 2:
                        pe.wait_ge(g1_done, u - 1)
                    for c in range(CT):
                        last = nc.tensor.matmul(ps_1[:, m, :], w1[:, c, m * P:(m + 1) * P], xnT[:, c, tok],
                                                start=(c == 0), stop=(c == CT - 1))
                    last.then_inc(l1_done, 1)

            def layer_2(n, blk):
                pe.wait_ge(g1_done, 4 * n + CT * (blk + 1))
                if n >= 1:
                    pe.wait_ge(g2_done, 2 * (n - 1) + blk + 1)
                for c in range(CT):
                    last = nc.tensor.matmul(ps_2[:, blk, :], w2[:, c, :], h1[:, n % 2, blk, c, :],
                                            start=(c == 0), stop=(c == CT - 1))
                last.then_inc(l2_done, 1)

            def layer_3(n):
                pe.wait_ge(g2_done, 2 * n + 2)
                if n >= 1:
                    pe.wait_ge(g3_done, n)
                for blk in range(2):
                    last = nc.tensor.matmul(ps_3[H3 * blk:H3 * (blk + 1), :], w3[:], h2[:, n % 2, blk, :],
                                            start=True, stop=True)
                last.then_inc(l3_done, 1)

            def layer_4(n):
                pe.wait_ge(g3_done, n + 1)
                for blk in range(2):
                    if n >= 1:
                        pe.wait_ge(th_done, 2 * (n - 1) + blk + 1)
                    nc.tensor.matmul(ps_4[:, blk, :], w4_wide[:, blk, :], h3[:], start=True,
                                     stop=True).then_inc(l4_done, 1)

            def global_net(stage):
                if stage == 0:
                    pe.wait_ge(glob_base, 4 + CT)
                    for c in range(CT):
                        last = nc.tensor.matmul(ps_g[:, 0:B], gw1[:, c, :], xsum[:, c, :], start=(c == 0),
                                                stop=(c == CT - 1))
                else:
                    pe.wait_ge(glob_act, stage)
                    if stage == 1:
                        last = nc.tensor.matmul(ps_g[0:H3, 0:B], gw2[:], gh1[:], start=True, stop=True)
                    else:
                        last = nc.tensor.matmul(ps_g[:, 0:B], gw3_wide[:], gh2[:], start=True, stop=True)
                last.then_inc(glob_mm, 1)

            pe.wait_ge(exp_done, NI * A_ROUND)
            pe.wait_ge(y_ready, NI * ENDS[BODY] + 1)
            pe.wait_ge(prep, PREP)
            for n in range(CYCLES * PAIRS + 2):
                if n < CYCLES * PAIRS:
                    layer_1(n, 0)
                if n >= 2:
                    layer_3(n - 2)
                if n < CYCLES * PAIRS:
                    layer_1(n, 1)
                if n >= 2:
                    layer_4(n - 2)
                if n < 3:
                    global_net(n)
                if 1 <= n <= CYCLES * PAIRS:
                    for blk in range(2):
                        layer_2(n - 1, blk)

            def turn_y(t):
                k = t // TPC
                if t % TPC == 0:
                    pe.wait_ge(yx_loaded[k % INPUTS], (k // INPUTS + 1) * 48)
                if t >= RING:
                    pe.wait_ge(yt_copied, t - RING + 1)
                for c in range(CT):
                    last = nc.tensor.transpose(ps_t[:, t % RING, c * P:(c + 1) * P], y_in[:, k % INPUTS, t % TPC, c, :],
                                               ident[:])
                last.then_inc(yt_ready, 1)

            pe.wait_ge(g2_done, 2 * CYCLES * PAIRS)
            pe.wait_ge(g3_done, CYCLES * PAIRS)
            for t in range(RING - 1):
                turn_y(t)
            for t in range(NT):
                if t + RING - 1 < NT:
                    turn_y(t + RING - 1)
                pe.wait_ge(yt_copied, t + 1)
                if t >= 2:
                    pe.wait_ge(res_ready, t - 1)
                if t % TPC == 0:
                    pe.wait_ge(upd_done, 2 * (2 * (CYCLES - 1) * PAIRS + t // TPC + 1))
                for c in range(CT):
                    nc.tensor.matmul(ps_y[:, t % 2, 0:C], yT[:, t % RING, c, :], wp_sb[:, c, :], start=(c == 0),
                                     stop=False)
                for c in range(CT):
                    last = nc.tensor.matmul(ps_y[:, t % 2, c * P:(c + 1) * P], xnT[:, c, t * P:(t + 1) * P],
                                            ident[:], start=False, stop=(c == CT - 1))
                last.then_inc(sum_ready, 1)


_FFN = ["cn_w1", "cn_b1", "cn_w2", "cn_b2", "cn_w3", "cn_b3", "cn_w4", "cn_b4", "gc_w1", "gc_b1", "gc_w2", "gc_b2",
        "gc_w3", "gc_b3", "adaptive_range"]


def rope_tables():
    half = HS // 2
    inv_freq = (np.float32(1.0) / np.float32(10000.0) ** (np.arange(half, dtype=np.float32) * np.float32(2.0)
                                                          / np.float32(HS))).astype(np.float32)
    ang = np.arange(T, dtype=np.float32)[:, None] * inv_freq[None, :]
    cos = np.repeat(np.cos(ang), 2, axis=1)
    sin = np.stack([-np.sin(ang), np.sin(ang)], axis=-1).reshape(T, HS)
    return [np.ascontiguousarray(a.astype(np.float32).reshape(TILES, P, HS).transpose(1, 0, 2)) for a in (cos, sin)]


def by_partition(v):
    return np.ascontiguousarray(v.reshape(CT, P).T)


def kernel(**inputs):
    import concourse.bacc as bacc
    from concourse.bass_utils import run_bass_kernel_spmd

    a = {k: np.ascontiguousarray(v) for k, v in inputs.items()}
    by_head = np.arange(P)
    by_dim = by_head.reshape(GROUPS, GH, HS).transpose(0, 2, 1).reshape(P)
    halves = [[P * (i % CT) + order for order in (by_dim, by_dim, by_head)] for i in range(NI)]
    wqkv = np.stack([np.concatenate([a[f"L0_attn_W{n}"][:, h] for n, h in zip("qkv", half)], axis=1)
                     for half in halves])
    bqkv = np.stack([np.concatenate([a[f"L0_attn_b{n}"][h] for n, h in zip("qkv", half)]) for half in halves])
    cos, sin = rope_tables()
    arrays = {
        "x": a["L0_attn_x"], "wqkv": wqkv, "bqkv": np.ascontiguousarray(np.broadcast_to(bqkv[:, None], (NI, P, QKV))),
        "wp": a["L0_attn_Wp"], "bp": by_partition(a["L0_attn_bp"]), "cos": cos, "sin": sin, "ident": np.eye(P, dtype=np.float32),
    }
    for n in _FFN:
        arrays[n] = a[f"L0_ffn_{n}"]
    arrays["cn_b1"] = by_partition(arrays["cn_b1"])
    nc = bacc.Bacc("TRN2", target_bir_lowering=False, num_devices=1)
    ap = {n: nc.dram_tensor(f"{n}_dram", v.shape, F32, kind="ExternalInput").ap() for n, v in arrays.items()}
    out = nc.dram_tensor("out_dram", (B, T, C), F32, kind="ExternalOutput").ap()
    y_dram = nc.dram_tensor("y_scratch", (NI, T, P), F32, kind="Internal").ap()
    build(nc, ap["x"], ap["wqkv"], ap["bqkv"], ap["wp"], ap["bp"], ap["cos"], ap["sin"], ap["ident"],
          {n: ap[n] for n in _FFN}, out, y_dram)
    r = run_bass_kernel_spmd(nc, [{f"{n}_dram": v for n, v in arrays.items()}], core_ids=[0])
    return r.results[0]["out_dram"]
```

```python
from contextlib import ExitStack

import numpy as np

import concourse.bass as bass
from concourse import mybir

ALU = mybir.AluOpType
ACT = mybir.ActivationFunctionType
AX_X = mybir.AxisListType.X
F32 = mybir.dt.float32
BF16 = mybir.dt.bfloat16

P = 128
B, T, C, NH = 2, 2048, 256, 16
HS = C // NH
CT = C // P
NI = B * CT
GH = 4
GROUPS = 2
TILES = T // P
QB = 512
CHUNKS = T // QB
TPC = QB // P
QKV = 3 * P
SPLITS = 3
SLOTS = [(0, 0), (1, 0), (2, 0), (0, 1), (1, 1), (0, 2)]
ROWS = HS * len(SLOTS)
SHIFT = ROWS
KROWS = ROWS + SPLITS
VW = HS + 1
SCALE = float(HS) ** -0.5
NEG = -1.0e30
EPS = 1e-5
H3 = 64
CYCLES = 3
PAIRS = B * T // (2 * QB)
RING = 3
INPUTS = 4
FIXED = 0.5
LEAD = 84
FIRST_PROJECTION = 9
DVE_LOW = 1
FIRST_STRIP = TPC + 5

STEPS = [(c, kt, max(0, kt * P - c * QB)) for c in range(CHUNKS) for kt in range(TPC * (c + 1))]
STRIPS = [(t, kb, min(QB, P * (t + 1) - QB * kb)) for t in range(TILES) for kb in range(t // TPC + 1)]
NS = len(STEPS)
BODY = GROUPS * NS


def strips_before(work):
    n, done = 0, 0
    while done < work:
        done += STRIPS[n % len(STRIPS)][2] // P + FIXED
        n += 1
    return n


def step_work(n):
    return sum((QB - lo) // P + FIXED for _, _, lo in STEPS[:n])


def strips_at(s):
    g, n = divmod(s, NS)
    a = strips_before(step_work(n) + LEAD) if n else strips_before(LEAD)
    b = strips_before(step_work(n + 1) + LEAD)
    return [(g + k // len(STRIPS), k % len(STRIPS)) for k in range(a, b)]


EARLY_STRIPS = [(0, k) for k in range(strips_before(LEAD))]


def last_of_chunk(k):
    t = STRIPS[k][0]
    last = k + 1 == len(STRIPS) or STRIPS[k + 1][0] != t
    return t // TPC if last and t % TPC == TPC - 1 else None


def round_jobs(last):
    at = [[] for _ in range(BODY + 1)]
    for s in range(BODY):
        for g, k in strips_at(s):
            c = last_of_chunk(k)
            if c is not None and not (last and g == GROUPS):
                at[min(s + 1, BODY)].append(("shift", g, c))
    n = 0
    for s in range(BODY):
        if ends_block(s):
            to = min(s + 2, BODY)
            while at[to] and to < BODY:
                to += 1
            at[to].append(("out", n))
            n += 1
    if not last:
        s = FIRST_PROJECTION
        for job in project_order():
            while at[s]:
                s += 1
            at[s].append(job)
            s += 1
    return at


def project_order():
    jobs = [("proj", 0)]
    for t in range(1, TILES):
        jobs += [("proj", t), ("turn", t - 1)]
    return jobs + [("turn", TILES - 1)]


def early_work():
    strips = list(range(len(EARLY_STRIPS)))
    work, shifts = [], []

    def strip():
        work.append(("strip", strips[0]))
        c = last_of_chunk(strips.pop(0))
        work.extend(shifts)
        shifts[:] = [] if c is None else [("shift", c)]

    for job in project_order():
        work.append(job)
        if job[0] == "turn" and job[1] >= FIRST_STRIP:
            for _ in range((job[1] - FIRST_STRIP) // TPC + 1):
                strip()
    while strips:
        strip()
    return work + shifts


def ring_distance(n):
    return RING if n >= A_ROUND % RING else A_ROUND % RING


def ends_block(s):
    c, kt, _ = STEPS[s % NS]
    return kt == TPC * (c + 1) - 1


def diagonal(s):
    c, kt, _ = STEPS[s % NS]
    return kt >= TPC * c


DIAG = [sum(diagonal(x) for x in range(s)) for s in range(BODY + 1)]
ENDS = [sum(ends_block(x) for x in range(s)) for s in range(BODY + 1)]
UNITS = [GH * sum(len(strips_at(x)) for x in range(s)) for s in range(BODY + 1)]
EARLY_UNITS = GH * len(EARLY_STRIPS)
A_ROUND = BODY * GH
assert A_ROUND == UNITS[BODY] and A_ROUND % RING > 0
EARLY = early_work()
EARLY_JOBS = sum(job != "strip" for job, _ in EARLY)
LOOP_JOBS, LAST_JOBS = round_jobs(False), round_jobs(True)
JOBS_A_ROUND = sum(map(len, LOOP_JOBS))
STACK_DMAS = len(SLOTS) * (1 + CHUNKS)
FIRST_STACK_DMAS = len(SLOTS) * 2
SHIFT_DMAS = SPLITS


def build(nc, x, wqkv, bqkv, wp, bp, cos, sin, ident_in, ffn, out, y_dram):
    x_tiles = x.rearrange("b (t p) c -> p (b t) c", p=P)
    out_tiles = out.rearrange("b (t p) c -> p (b t) c", p=P)
    NT = B * TILES
    with ExitStack() as ctx:
        def sem(name):
            return ctx.enter_context(nc.semaphore(name))

        def sb(scope, name, shape, dt=F32):
            return scope.enter_context(nc.sbuf_tensor(name, shape, dt))

        def pb(scope, name, shape):
            return scope.enter_context(nc.psum_tensor(name, shape, F32))

        xnT = sb(ctx, "xnT", [P, CT, B * T])
        ident = sb(ctx, "ident", [P, P])
        wp_sb = sb(ctx, "wp_sb", [P, CT, C])
        bp_sb = sb(ctx, "bp_sb", [P, CT])
        w1 = sb(ctx, "w1", [P, CT, C])
        b1 = sb(ctx, "b1", [P, CT])
        w2 = sb(ctx, "w2", [P, CT, P])
        b2 = sb(ctx, "b2", [P, 1])
        w3 = sb(ctx, "w3", [P, H3])
        b3 = sb(ctx, "b3", [P, 1])
        w4 = sb(ctx, "w4", [P, 1])
        w4_wide = sb(ctx, "w4_wide", [P, 2, P])
        b4 = sb(ctx, "b4", [P, 1])
        gw1 = sb(ctx, "gw1", [P, CT, P])
        gb1 = sb(ctx, "gb1", [P, 1])
        gw2 = sb(ctx, "gw2", [P, H3])
        gb2 = sb(ctx, "gb2", [H3, 1])
        gw3 = sb(ctx, "gw3", [H3, 1])
        gw3_wide = sb(ctx, "gw3_wide", [H3, P])
        gb3 = sb(ctx, "gb3", [P, 1])
        ar = sb(ctx, "ar", [P, 1])
        sign = sb(ctx, "sign", [P, 1])
        swing = sb(ctx, "swing", [P, 1])
        base = sb(ctx, "base", [P, B])
        xsum = sb(ctx, "xsum", [P, CT, B])
        gh1 = sb(ctx, "gh1", [P, B])
        gh2 = sb(ctx, "gh2", [H3, B])
        gtanh = sb(ctx, "gtanh", [P, B])

        stats = sb(ctx, "stats", [P, NT, 6])
        meanvar = sb(ctx, "meanvar", [P, NT, 2])
        std = sb(ctx, "std", [P, B, TILES])
        rstd = sb(ctx, "rstd", [P, B, TILES])

        with ExitStack() as s1:
            x_in = sb(s1, "x_in", [P, NT, C])
            ps_x = pb(s1, "ps_x", [P, 2, QB])

        with ExitStack() as s2:
            qst = [sb(s2, f"qst{g}", [P, CHUNKS, GH, QB], BF16) for g in range(GROUPS)]
            kst = [sb(s2, f"kst{g}", [P, GH, T], BF16) for g in range(GROUPS)]
            parts = sb(s2, "parts", [P, 2, SPLITS, T], BF16)
            probs = sb(s2, "probs", [P, 2, GH, QB])
            vcur = [sb(s2, f"vcur{g}", [P, TILES, GH, VW]) for g in range(GROUPS)]
            vnext = sb(s2, "vnext", [P, GROUPS, TILES, GH, VW])
            xwin = sb(s2, "xwin", [P, 2, CT, QB])
            wcur = sb(s2, "wcur", [P, CT, QKV])
            bcur = sb(s2, "bcur", [P, QKV])
            cos_sb = sb(s2, "cos_sb", [P, TILES, HS])
            sin_sb = sb(s2, "sin_sb", [P, TILES, HS])
            qk_in = sb(s2, "qk_in", [P, 2, 2 * P])
            qk_cos = sb(s2, "qk_cos", [P, 2 * P])
            qk_rot = sb(s2, "qk_rot", [P, 2, 2 * P])
            rest = sb(s2, "rest", [P, 2, 2, P])
            mask = sb(s2, "mask", [P, QB])
            strip_max = sb(s2, "strip_max", [P, GH, TILES, CHUNKS])
            neg_max = sb(s2, "neg_max", [P, 2, GH, TPC])
            mparts = sb(s2, "mparts", [GH * TPC, 2, SPLITS, P], BF16)
            mrest = sb(s2, "mrest", [GH * TPC, P])
            o_sb = sb(s2, "o_sb", [P, 2, QB])
            recip = sb(s2, "recip", [P, TPC * GH])
            y_sb = sb(s2, "y_sb", [P, 2, TPC * GH * HS])
            ps_s = pb(s2, "ps_s", [P, RING, QB])
            ps_m = pb(s2, "ps_m", [P, RING, QB])
            ps_o = pb(s2, "ps_o", [P, QB])
            ps_j = pb(s2, "ps_j", [P, QB])

        with ExitStack() as s3:
            h1 = sb(s3, "h1", [P, 2, 2, CT, QB])
            h2 = sb(s3, "h2", [P, 2, 2, QB])
            h3 = sb(s3, "h3", [P, QB])
            th = sb(s3, "th", [P, 2, QB])
            coup = sb(s3, "coup", [P, 2, QB])
            prod = sb(s3, "prod", [P, 2, CT, QB])
            y_in = sb(s3, "y_in", [P, INPUTS, TPC, CT, P])
            x_res = sb(s3, "x_res", [P, INPUTS, TPC, C])
            yT = sb(s3, "yT", [P, RING, CT, P])
            res = sb(s3, "res", [P, 2, TPC, C])
            with ExitStack() as s4:
                ps_1 = pb(s4, "ps_1", [P, 2, QB])
                ps_2 = pb(s4, "ps_2", [P, 2, QB])
                ps_3 = pb(s4, "ps_3", [P, QB])
                ps_4 = pb(s4, "ps_4", [P, 2, QB])
                ps_g = pb(s4, "ps_g", [P, QB])
            with ExitStack() as s4:
                ps_t = pb(s4, "ps_t", [P, RING, QB])
                ps_y = pb(s4, "ps_y", [P, 2, QB])
                ps_f = pb(s4, "ps_f", [P, 2, QB])

        x_loaded = [sem(f"x_loaded{k}") for k in range(NT // TPC)]
        ident_loaded, weights_loaded, rope_loaded = sem("ident_loaded"), sem("weights_loaded"), sem("rope_loaded")
        stats_done, var_done, std_done, rstd_done = sem("stats_done"), sem("var_done"), sem("std_done"), sem("rstd_done")
        xn_ready, xt_ready, xt_copied = sem("xn_ready"), sem("xt_ready"), sem("xt_copied")
        set_up, pool_ones, zeros_set = sem("set_up"), sem("pool_ones"), sem("zeros_set")
        w_loaded = sem("w_loaded")
        win_loaded = [sem("win_loaded0"), sem("win_loaded1")]
        job_ready = sem("job_ready")
        v_ready, y_ready = sem("v_ready"), sem("y_ready")
        qk_ready, cos_done, rot_done = sem("qk_ready"), sem("cos_done"), sem("rot_done")
        hi_ready, rest_ready, mid_done, parts_ready = sem("hi_ready"), sem("rest_ready"), sem("mid_done"), sem("parts_ready")
        first_stack = [sem(f"first_stack{c}") for c in range(CHUNKS)]
        stack_loaded = [sem("stack_loaded0"), sem("stack_loaded1")]
        v_loaded = [sem("v_loaded0"), sem("v_loaded1")]
        max_ready, max_used = sem("max_ready"), sem("max_used")
        neg_ready, mhi_ready, mrest_ready, mmid_ready, mparts_ready = (sem(n) for n in (
            "neg_ready", "mhi_ready", "mrest_ready", "mmid_ready", "mparts_ready"))
        shift_loaded = [sem(f"shift_loaded{c}") for c in range(CHUNKS)]
        scores_ready, exp_done, mask_done, pv_done = sem("scores_ready"), sem("exp_done"), sem("mask_done"), sem("pv_done")
        o_copied, o_turned = sem("o_copied"), sem("o_turned")
        y_stored = [sem("y_stored0"), sem("y_stored1")]
        prep = sem("prep")
        l1_done, l2_done, l3_done, l4_done = sem("l1_done"), sem("l2_done"), sem("l3_done"), sem("l4_done")
        g1_done, g2_done, g3_done, th_done = sem("g1_done"), sem("g2_done"), sem("g3_done"), sem("th_done")
        coup_done, prod_done, upd_done = sem("coup_done"), sem("prod_done"), sem("upd_done")
        glob_mm, glob_act, glob_base = sem("glob_mm"), sem("glob_act"), sem("glob_base")
        yx_loaded = [sem(f"yx_loaded{k}") for k in range(INPUTS)]
        yt_ready, yt_copied, sum_ready, res_ready = sem("yt_ready"), sem("yt_copied"), sem("sum_ready"), sem("res_ready")
        turned_back, half_sum = sem("turned_back"), sem("half_sum")
        out_stored = [sem("out_stored0"), sem("out_stored1")]

        def column(v):
            return v.rearrange("(p o) -> p o", o=1)

        weights = [
            (wp_sb[:], wp.rearrange("(c p) n -> p c n", p=P)), (bp_sb[:], bp),
            (w1[:], ffn["cn_w1"].rearrange("(c p) n -> p c n", p=P)), (b1[:], ffn["cn_b1"]),
            (w2[:], ffn["cn_w2"].rearrange("(c p) n -> p c n", p=P)), (b2[:], column(ffn["cn_b2"])),
            (w3[:], ffn["cn_w3"]), (b3[0:H3], column(ffn["cn_b3"])), (b3[H3:P], column(ffn["cn_b3"])),
            (w4[0:H3], ffn["cn_w4"]), (w4[H3:P], ffn["cn_w4"]),
            (b4[:], ffn["cn_b4"].partition_broadcast(P)),
            (gw1[:], ffn["gc_w1"].rearrange("(c p) n -> p c n", p=P)), (gb1[:], column(ffn["gc_b1"])),
            (gw2[:], ffn["gc_w2"]), (gb2[:], column(ffn["gc_b2"])),
            (gw3[:], ffn["gc_w3"]), (gb3[:], ffn["gc_b3"].partition_broadcast(P)),
            (ar[:], ffn["adaptive_range"].partition_broadcast(P)),
        ]
        PREP = 7

        def rounds(eng, body):
            with eng.Fori(0, NI - 1) as i:
                body(i, LOOP_JOBS, False)
            body(NI - 1, LAST_JOBS, True)

        def jobs_before(i, jobs, s):
            return EARLY_JOBS + i * JOBS_A_ROUND + sum(map(len, jobs[:s]))

        def unit_at(i, s):
            return (i + 1) * A_ROUND + (EARLY_UNITS - A_ROUND + UNITS[s])

        def spread(units):
            cut = [len(units) * quarters // 4 for quarters in QUARTERS]
            return [units[a:b] for a, b in zip(cut, cut[1:])]

        VALUES_AT = 4
        QUARTERS = (0, 0, 1, 2, 3, 3, 4)
        DVE_AHEAD = 0

        def early_bank(number):
            return ps_j if number % 2 == 0 else ps_s[:, RING - 1]

        def wait_alone(eng, semaphore, value):
            eng.wait_ge(semaphore, value)
            eng.nop(nofuse=True)

        block = ctx.enter_context(nc.Block())

        @block.sync
        def _(sp):
            def load_x(k):
                sp.dma_start(x_in[:, k * TPC:(k + 1) * TPC, :],
                             x_tiles[:, k * TPC:(k + 1) * TPC, :]).then_inc(x_loaded[k], 16)

            for k in range(CHUNKS):
                load_x(k)
            sp.dma_start(ident[:], ident_in).then_inc(ident_loaded, 16)

            def load_weights(r):
                sp.dma_start(wcur[:], wqkv[bass.ds(r, 1), :, :].rearrange("i (c p) n -> p (i c) n", p=P)
                             ).then_inc(w_loaded, 16)
                sp.dma_start(bcur[:], bqkv[bass.ds(r, 1), :, :].rearrange("i p n -> (i p) n")).then_inc(w_loaded, 16)

            load_weights(0)
            sp.dma_start(cos_sb[:], cos).then_inc(rope_loaded, 16)
            sp.dma_start(sin_sb[:], sin).then_inc(rope_loaded, 16)
            for k in range(CHUNKS, NT // TPC):
                load_x(k)
            for dst, src in weights:
                sp.dma_start(dst, src).then_inc(weights_loaded, 16)

            def load_window(r, cc):
                sp.dma_start(xwin[:, cc % 2], xnT[:, :, bass.ds((r // CT) * T + cc * QB, QB)]
                             ).then_inc(win_loaded[cc % 2], 16)

            def load_stack(g):
                for n, (_, kpart) in enumerate(SLOTS):
                    sp.dma_start(kst[g][HS * n:HS * (n + 1)],
                                 parts[heads(g), 1, kpart, :]).then_inc(stack_loaded[g], 16)
                for c in range(CHUNKS):
                    load_stack_q(g, c, stack_loaded[g])

            def heads(g):
                return slice(HS * GH * g, HS * GH * (g + 1))

            def load_stack_q(g, c, done):
                for n, (qpart, _) in enumerate(SLOTS):
                    sp.dma_start(qst[g][HS * n:HS * (n + 1), c],
                                 parts[heads(g), 0, qpart, c * QB:(c + 1) * QB]).then_inc(done, 16)

            def load_first_stack(c):
                for n, (_, kpart) in enumerate(SLOTS):
                    sp.dma_start(kst[0][HS * n:HS * (n + 1), :, c * QB:(c + 1) * QB],
                                 parts[heads(0), 1, kpart, c * QB:(c + 1) * QB]).then_inc(first_stack[c], 16)
                load_stack_q(0, c, first_stack[c])

            def load_v(g):
                sp.dma_start(vcur[g][:].rearrange("p t h d -> p (t h d)"),
                             vnext[:, g].rearrange("p t h d -> p (t h d)")).then_inc(v_loaded[g], 16)

            def load_shift(g, c):
                for p in range(SPLITS):
                    sp.dma_start(qst[g % GROUPS][SHIFT + p:SHIFT + p + 1, c],
                                 mparts[:, c % 2, p, :]).then_inc(shift_loaded[c], 16)

            for cc in (0, 1):
                sp.wait_ge(xt_copied, CT * (cc + 1))
                load_window(0, cc)
            for job, t in EARLY:
                c = t // TPC
                if job == "proj" and t in (TPC - 1, 2 * TPC - 1):
                    sp.wait_ge(qk_ready, TPC * (c + 1))
                    sp.wait_ge(xt_copied, CT * (c + 3))
                    load_window(0, c + 2)
                elif job == "turn" and t % TPC == TPC - 1:
                    sp.wait_ge(parts_ready, TPC * (c + 1))
                    if c == 0:
                        sp.wait_ge(xt_ready, CT * CHUNKS)
                    load_first_stack(c)
                elif job == "shift":
                    sp.wait_ge(mparts_ready, t + 1)
                    load_shift(0, t)
            sp.wait_ge(v_ready, TILES)
            load_v(0)

            def store(k):
                sp.wait_ge(res_ready, TPC * (k + 1))
                sp.dma_start(out_tiles[:, k * TPC:(k + 1) * TPC, :], res[:, k % 2]).then_inc(out_stored[k % 2], 16)

            def body(i, jobs, last):
                if not last:
                    sp.wait_ge(v_ready, (i + 1) * TILES)
                    load_weights(i + 1)
                    for cc in (0, 1):
                        load_window(i + 1, cc)
                sp.wait_ge(scores_ready, i * A_ROUND + GH)
                load_stack(1)
                pending = []
                for s in range(BODY + 1):
                    if s == 1:
                        sp.wait_ge(pv_done, i * BODY + 1)
                        load_v(1)
                    for job in pending:
                        if job[0] == "shift":
                            sp.wait_ge(mparts_ready, i * GROUPS * CHUNKS + CHUNKS * job[1] + job[2] + 1)
                            load_shift(job[1], job[2])
                        elif job[0] == "out":
                            store_y(i, job[1])
                        elif job[0] == "proj" and job[1] in (TPC - 1, 2 * TPC - 1):
                            cc = job[1] // TPC + 2
                            sp.wait_ge(qk_ready, (i + 1) * TILES + TPC * (cc - 1))
                            load_window(i + 1, cc)
                        elif job == ("turn", TILES - 1):
                            sp.wait_ge(scores_ready, i * A_ROUND + GH * NS)
                            sp.wait_ge(parts_ready, (i + 2) * TILES)
                            load_stack(0)
                            sp.wait_ge(pv_done, i * BODY + NS)
                            load_v(0)
                    pending = jobs[s]
                for job in pending:
                    store_y(i, job[1])

            def store_y(i, n):
                sp.wait_ge(y_ready, i * ENDS[BODY] + n + 2)
                g, c = divmod(n, CHUNKS)
                sp.dma_start(
                    y_dram[bass.ds(i, 1), c * QB:(c + 1) * QB, g * GH * HS:(g + 1) * GH * HS]
                    .rearrange("i (t p) d -> p (i t) d", p=P),
                    y_sb[:, n % 2].rearrange("p (t d) -> p t d", t=TPC)).then_inc(y_stored[n % 2], 16)

            rounds(sp, body)

            for p in range(2):
                sp.wait_ge(y_stored[p], NI * ENDS[BODY] // 2 * 16 + 1)
            sp.wait_ge(pv_done, NI * BODY)
            def load(k):
                b, c = divmod(k, CHUNKS)
                at = k % INPUTS
                for half in range(CT):
                    sp.dma_start(y_in[:, at, :, half, :], y_dram[CT * b + half, c * QB:(c + 1) * QB, :]
                                 .rearrange("(t p) d -> p t d", p=P)).then_inc(yx_loaded[at], 16)
                sp.dma_start(x_res[:, at], x_tiles[:, k * TPC:(k + 1) * TPC, :]).then_inc(yx_loaded[at], 16)

            for k in range(INPUTS):
                load(k)
            for k in range(NT // TPC):
                store(k)
                if k + INPUTS < NT // TPC:
                    load(k + INPUTS)
            for p in range(2):
                sp.wait_ge(out_stored[p], NT // TPC // 2 * 16)

        @block.gpsimd
        def _(pool):
            nc.gpsimd.memset(mask[:], 0.0).then_inc(set_up, 1)
            pool.wait_ge(set_up, 1)
            nc.gpsimd.affine_select(out=mask[:, QB - P:], in_=mask[:, QB - P:], pattern=[[-1, P]],
                                    compare_op=ALU.is_ge, fill=NEG, base=0,
                                    channel_multiplier=1).then_inc(set_up, 1)
            nc.gpsimd.memset(vnext[:], 1.0).then_inc(pool_ones, 1)
            for g in range(GROUPS):
                pool.wait_ge(pool_ones, g + 1)
                nc.gpsimd.memset(kst[g][SHIFT:KROWS], 1.0).then_inc(pool_ones, 1)
            pool.wait_ge(rope_loaded, 32)

            def rotate(r, t):
                n = r * TILES + t
                src, dst, cosines = (a.rearrange("p (g d h) -> p g d h", d=HS, h=GH) for a in (
                    qk_in[:, t % 2], qk_rot[:, t % 2], qk_cos[:]))

                def table(tab, a, step):
                    return tab[:, t:t + 1, a::step].rearrange("p g (d h) -> p g d h", h=1).broadcast_to(
                        [P, 2 * GROUPS, HS // step, GH])

                if not (isinstance(n, int) and n == 0):
                    pool.wait_ge(rot_done, n)
                pool.wait_ge(qk_ready, n + 1)
                nc.gpsimd.tensor_tensor(cosines, src,
                                        table(cos_sb, 0, 1), ALU.mult).then_inc(cos_done, 1)
                if not (isinstance(r, int) and r == 0 and t < 2):
                    pool.wait_ge(rest_ready, n - 1)
                for a in (0, 1):
                    nc.gpsimd.tensor_tensor(dst[:, :, a::2, :], src[:, :, 1 - a::2, :],
                                            table(sin_sb, a, 2), ALU.mult).then_inc(cos_done, 1)
                pool.wait_ge(cos_done, 3 * (n + 1))
                nc.gpsimd.tensor_tensor(qk_rot[:, t % 2], qk_rot[:, t % 2], qk_cos[:],
                                        ALU.add).then_inc(rot_done, 1)

            def split(r, t):
                n = r * TILES + t
                at = slice(t * P, (t + 1) * P)
                if not (isinstance(r, int) and r == 0):
                    wait_alone(pool, rest_ready, n + 1)
                    nc.gpsimd.tensor_copy(parts[:, :, 1, at], rest[:, t % 2]).then_inc(mid_done, 1)
                pool.wait_ge(mid_done, n + 1)
                if isinstance(r, int) and r == 0 and t == DVE_LOW:
                    pool.wait_ge(parts_ready, DVE_LOW)
                nc.gpsimd.tensor_tensor(parts[:, :, 2, at], rest[:, t % 2], parts[:, :, 1, at],
                                        ALU.subtract).then_inc(parts_ready, 1)

            def mask_step(i, s):
                lo = STEPS[s % NS][2]
                wait_alone(pool, exp_done, i * A_ROUND + GH * (s + 1))
                blockp = probs[:, s % 2, :, lo:lo + P]
                nc.gpsimd.affine_select(out=blockp, in_=blockp, pattern=[[0, GH], [1, P]],
                                        compare_op=ALU.is_ge, fill=0.0, base=0,
                                        channel_multiplier=-1).then_inc(mask_done, 1)

            for job, t in project_order():
                if job == "proj":
                    rotate(0, t)
                elif t >= DVE_LOW:
                    split(0, t)
            mask_step(0, 0)

            def body(i, jobs, last):
                for s in range(BODY):
                    if s + 1 < BODY:
                        if diagonal(s + 1):
                            mask_step(i, s + 1)
                    elif not last:
                        mask_step(i + 1, 0)
                    for job in jobs[s]:
                        if job[0] == "proj":
                            rotate(i + 1, job[1])
                        elif job[0] == "turn":
                            split(i + 1, job[1])

            rounds(pool, body)

        @block.scalar
        def _(act):
            def root(b):
                act.wait_ge(var_done, b + 1)
                nc.scalar.activation(std[:, b, :], std[:, b, :], ACT.Sqrt).then_inc(std_done, 1)

            def copy_xt(k):
                for c in range(CT):
                    n = k * CT + c
                    act.wait_ge(xt_ready, n + 1)
                    nc.scalar.activation(xnT[:, c, k * QB:(k + 1) * QB], ps_x[:, n % 2, :],
                                         ACT.Copy).then_inc(xt_copied, 1)

            root(0)
            for k in range(CHUNKS):
                copy_xt(k)

            def exps(i, s):
                lo = STEPS[s % NS][2]
                for h in range(GH):
                    n = GH * s + h
                    act.wait_ge(scores_ready, i * A_ROUND + n + 1)
                    if h == 0 and s >= 2:
                        act.wait_ge(pv_done, i * BODY + s - 1)
                    elif h == 0 and s == 0 and not (isinstance(i, int) and i == 0):
                        act.wait_ge(pv_done, i * BODY - 1)
                    nc.scalar.activation(probs[:, s % 2, h, lo:], ps_s[:, n % RING, lo:], ACT.Exp,
                                         scale=SCALE).then_inc(exp_done, 1)

            def high(r, t, number, bank=ps_j):
                act.wait_ge(job_ready, number + 1)
                if t == 0 and not (isinstance(r, int) and r == 0):
                    act.wait_ge(stack_loaded[1], r * STACK_DMAS * 16)
                nc.scalar.activation(parts[:, :, 0, t * P:(t + 1) * P],
                                     bank[:, 0:2 * P].rearrange("p (a n) -> p a n", a=2),
                                     ACT.Copy).then_inc(hi_ready, 1)

            def shift_high(g, c, number, bank=ps_j):
                act.wait_ge(job_ready, number + 1)
                if c >= 2:
                    act.wait_ge(shift_loaded[c - 2], (g + 1) * SHIFT_DMAS * 16)
                elif not (isinstance(g, int) and g == 0):
                    act.wait_ge(shift_loaded[c + 2], g * SHIFT_DMAS * 16)
                nc.scalar.activation(mparts[:, c % 2, 0, :], bank[0:GH * TPC, 0:P],
                                     ACT.Copy).then_inc(mhi_ready, 1)

            def copy_out(i, s):
                n = ENDS[s]
                act.wait_ge(pv_done, i * BODY + s + 1)
                act.wait_ge(o_turned, i * ENDS[BODY] + max(n - 1, 0) + 1)
                nc.scalar.activation(o_sb[:, n % 2], ps_o[:], ACT.Copy).then_inc(o_copied, 1)

            number = 0
            for job, t in EARLY:
                if job == "turn":
                    high(0, t, number, early_bank(number))
                    act.wait_ge(rest_ready, t + 1)
                    nc.scalar.activation(parts[:, :, 1, t * P:(t + 1) * P], rest[:, t % 2],
                                         ACT.Copy).then_inc(mid_done, 1)
                    if t == TPC - 1:
                        root(1)
                    elif TPC < t <= 2 * TPC:
                        copy_xt(t - 1)
                elif job == "shift":
                    shift_high(0, t, number, early_bank(number))
                number += job != "strip"
            exps(0, 0)

            def body(i, jobs, last):
                for s in range(BODY + 1):
                    if s + 1 < BODY:
                        exps(i, s + 1)
                    elif s + 1 == BODY and not last:
                        exps(i + 1, 0)
                    for n, job in enumerate(jobs[s]):
                        number = jobs_before(i, jobs, s) + n
                        if job[0] == "turn":
                            high(i + 1, job[1], number)
                        elif job[0] == "shift":
                            shift_high(i * GROUPS + job[1], job[2], number)
                    if s < BODY and ends_block(s):
                        copy_out(i, s)

            rounds(act, body)

            for p in range(2):
                act.wait_ge(y_stored[p], NI * ENDS[BODY] // 2 * 16 + 1)

            def gelu(out_, in_, bias, done):
                nc.scalar.activation(out_, in_, ACT.Gelu, bias=bias).then_inc(done, 1)

            def gelu_1(n, blk):
                for m in range(CT):
                    u = 4 * n + CT * blk + m
                    act.wait_ge(l1_done, u + 1)
                    if n >= 2:
                        act.wait_ge(l2_done, 2 * (n - 2) + blk + 1)
                    gelu(h1[:, n % 2, blk, m, :], ps_1[:, m, :], b1[:, m:m + 1], g1_done)

            def global_net(stage):
                act.wait_ge(glob_mm, stage + 1)
                if stage == 0:
                    gelu(gh1[:], ps_g[:, 0:B], gb1[:, 0:1], glob_act)
                elif stage == 1:
                    gelu(gh2[:], ps_g[0:H3, 0:B], gb2[:, 0:1], glob_act)
                else:
                    nc.scalar.activation(gtanh[:], ps_g[:, 0:B], ACT.Tanh, bias=gb3[:, 0:1],
                                         scale=0.5).then_inc(glob_act, 1)

            act.wait_ge(weights_loaded, 16 * len(weights))
            act.wait_ge(prep, PREP)
            for n in range(CYCLES * PAIRS + 2):
                if n < CYCLES * PAIRS:
                    gelu_1(n, 0)
                if n >= 2:
                    m = n - 2
                    act.wait_ge(l3_done, m + 1)
                    if m >= 1:
                        act.wait_ge(l4_done, 2 * m)
                    gelu(h3[:], ps_3[:], b3[:, 0:1], g3_done)
                if n < CYCLES * PAIRS:
                    gelu_1(n, 1)
                if n >= 2:
                    for blk in range(2):
                        act.wait_ge(l4_done, 2 * m + blk + 1)
                        if m >= 1:
                            act.wait_ge(coup_done, 2 * (m - 1) + blk + 1)
                        nc.scalar.activation(th[:, blk, :], ps_4[:, blk, :], ACT.Tanh, bias=b4[:, 0:1],
                                             scale=0.5).then_inc(th_done, 1)
                if n < 3:
                    global_net(n)
                if 1 <= n <= CYCLES * PAIRS:
                    m = n - 1
                    for blk in range(2):
                        act.wait_ge(l2_done, 2 * m + blk + 1)
                        if m >= 2:
                            act.wait_ge(l3_done, m - 1)
                        gelu(h2[:, m % 2, blk, :], ps_2[:, blk, :], b2[:, 0:1], g2_done)

            for t in range(NT):
                act.wait_ge(yt_ready, t + 1)
                if t >= RING:
                    act.wait_ge(sum_ready, t - RING + 1)
                nc.scalar.activation(yT[:, t % RING], ps_t[:, t % RING, 0:C].rearrange("p (c n) -> p c n", c=CT),
                                     ACT.Copy).then_inc(yt_copied, 1)

        @block.vector
        def _(dve):
            def norm_stats(k):
                dve.wait_ge(x_loaded[k], 16)
                for t in range(k * TPC, (k + 1) * TPC):
                    nc.vector.bn_stats(stats[:, t, :], x_in[:, t, :]).then_inc(stats_done, 1)

            def norm_variance(b):
                for n in range(TILES):
                    t = b * TILES + n
                    dve.wait_ge(stats_done, 2 * TILES * b + n + 1)
                    nc.vector.bn_aggr(meanvar[:, t, :], stats[:, t, :]).then_inc(stats_done, 1)
                dve.wait_ge(stats_done, 2 * TILES * (b + 1))
                nc.vector.tensor_scalar(std[:, b, :], meanvar[:, b * TILES:(b + 1) * TILES, 1], EPS, None,
                                        ALU.add).then_inc(var_done, 1)

            def norm_root(b):
                dve.wait_ge(std_done, b + 1)
                nc.vector.reciprocal(rstd[:, b, :], std[:, b, :]).then_inc(rstd_done, 1)
                dve.wait_ge(rstd_done, b + 1)

            def norm_apply(k):
                for t in range(k * TPC, (k + 1) * TPC):
                    nc.vector.tensor_scalar(x_in[:, t, :], x_in[:, t, :], meanvar[:, t, 0:1],
                                            rstd[:, t // TILES, t % TILES:t % TILES + 1], ALU.subtract,
                                            ALU.mult).then_inc(xn_ready, 1)

            for k in range(CHUNKS):
                norm_stats(k)
            norm_variance(0)
            norm_root(0)
            for k in range(CHUNKS):
                norm_apply(k)

            def constants():
                dve.wait_ge(weights_loaded, 16 * len(weights))
                nc.vector.memset(sign[0:H3], 1.0).then_inc(prep, 1)
                nc.vector.memset(sign[H3:P], -1.0).then_inc(prep, 1)
                nc.vector.memset(w4_wide[:], 0.0).then_inc(prep, 1)
                dve.wait_ge(prep, 3)
                nc.vector.tensor_scalar(b4[:], b4[:], 0.5, None, ALU.mult).then_inc(prep, 1)
                nc.vector.tensor_scalar(gb3[:], gb3[:], 0.5, None, ALU.mult).then_inc(prep, 1)
                for blk in range(2):
                    rows = slice(H3 * blk, H3 * (blk + 1))
                    nc.vector.tensor_scalar(w4_wide[rows, blk, :], w4_wide[rows, blk, :], w4[rows, 0:1], None,
                                            ALU.add).then_inc(prep, 1)
                nc.vector.tensor_scalar(swing[:], ar[:], sign[:, 0:1], 0.3, ALU.mult, ALU.mult).then_inc(glob_base, 1)
                nc.vector.memset(gw3_wide[:], 0.0).then_inc(glob_base, 1)
                dve.wait_ge(glob_base, 2)
                nc.vector.tensor_scalar(gw3_wide[:], gw3_wide[:], gw3[:, 0:1], None, ALU.add).then_inc(glob_base, 1)

            nc.vector.memset(ps_o[:], 0.0).then_inc(zeros_set, 1)
            dve.wait_ge(pool_ones, 3)
            dve.wait_ge(zeros_set, 1)
            for free, buf in ((o_turned, o_sb[:, 0, 0:1]), (y_ready, recip[:, 0:1]),
                              (y_stored[0], y_sb[:, 0, 0:1]), (y_stored[1], y_sb[:, 1, 0:1])):
                nc.vector.memset(buf, 0.0).then_inc(free, 1)

            def project(r, t, number, bank=ps_j):
                n = r * TILES + t
                first = isinstance(r, int) and r == 0
                dve.wait_ge(job_ready, number + 1)
                if not (first and t < 2):
                    dve.wait_ge(rot_done, n - 1)
                nc.vector.tensor_tensor(qk_in[:, t % 2], bank[:, 0:2 * P], bcur[:, 0:2 * P],
                                        ALU.add).then_inc(qk_ready, 1)
                if t == 0 and not first:
                    for g in range(GROUPS):
                        dve.wait_ge(v_loaded[g], r * 16)
                nc.vector.tensor_tensor(vnext[:, :, t, :, 0:HS],
                                        bank[:, 2 * P:3 * P].rearrange("p (g h d) -> p g h d", g=GROUPS, h=GH),
                                        bcur[:, 2 * P:3 * P].rearrange("p (g h d) -> p g h d", g=GROUPS, h=GH),
                                        ALU.add).then_inc(v_ready, 1)

            def remainder(r, t, bank=ps_j):
                n = r * TILES + t
                dve.wait_ge(hi_ready, n + 1)
                if not (isinstance(r, int) and r == 0 and t < 2):
                    dve.wait_ge(parts_ready, n - 1)
                nc.vector.tensor_tensor(rest[:, t % 2], bank[:, 0:2 * P].rearrange("p (a n) -> p a n", a=2),
                                        parts[:, :, 0, t * P:(t + 1) * P], ALU.subtract).then_inc(rest_ready, 1)

            def strip(g, k, h, unit, place):
                t, kb, w = STRIPS[k]
                at = strip_max[:, h, t, kb:kb + 1]
                scores = ps_m[:, place % RING, 0:w]
                if kb == t // TPC:
                    dve.wait_ge(set_up, 2)
                    wait_alone(dve, max_ready, unit + 1)
                else:
                    dve.wait_ge(max_ready, unit + 1)
                if kb == t // TPC:
                    nc.vector.tensor_tensor_reduce(scores, scores, mask[:, QB - w:], 1.0, NEG,
                                                   ALU.add, ALU.max, at).then_inc(max_used, 1)
                else:
                    nc.vector.tensor_reduce(at, scores, AX_X, ALU.max).then_inc(max_used, 1)

            def chunk_max(c, units):
                dve.wait_ge(max_used, units)
                nc.vector.tensor_reduce(neg_max[:, c % 2], strip_max[:, :, TPC * c:TPC * (c + 1), 0:c + 1],
                                        AX_X, ALU.max, negate=True).then_inc(neg_ready, 1)

            def shift(c, n, bank=ps_j):
                m = mparts[:, c % 2]
                dve.wait_ge(mhi_ready, n + 1)
                nc.vector.tensor_tensor(mrest[:], bank[0:GH * TPC, 0:P], m[:, 0, :],
                                        ALU.subtract).then_inc(mrest_ready, 1)
                dve.wait_ge(mrest_ready, n + 1)
                nc.vector.tensor_copy(m[:, 1, :], mrest[:]).then_inc(mmid_ready, 1)
                dve.wait_ge(mmid_ready, n + 1)
                nc.vector.tensor_tensor(m[:, 2, :], mrest[:], m[:, 1, :], ALU.subtract).then_inc(mparts_ready, 1)

            def normalise(i, n, number):
                turned = ps_j[:].rearrange("p (a d) -> p a d", d=2 * HS)
                dve.wait_ge(job_ready, number + 1)
                nc.vector.reciprocal(recip[:].rearrange("p (a d) -> p a d", d=1),
                                     turned[:, :, HS:VW]).then_inc(o_turned, 1)
                dve.wait_ge(o_turned, i * ENDS[BODY] + n + 2)
                dve.wait_ge(y_stored[n % 2], (i * (ENDS[BODY] // 2) + n // 2) * 16 + 1)
                nc.vector.tensor_tensor(y_sb[:, n % 2].rearrange("p (a d) -> p a d", d=HS), turned[:, :, 0:HS],
                                        recip[:].rearrange("p (a d) -> p a d", d=1)
                                        .broadcast_to([P, TPC * GH, HS]), ALU.mult).then_inc(y_ready, 1)

            def low(t):
                at = slice(t * P, (t + 1) * P)
                dve.wait_ge(mid_done, t + 1)
                nc.vector.tensor_tensor(parts[:, :, 2, at], rest[:, t % 2], parts[:, :, 1, at],
                                        ALU.subtract).then_inc(parts_ready, 1)

            unit = number = 0
            for job, t in EARLY:
                if job == "proj":
                    project(0, t, number, early_bank(number))
                elif job == "turn":
                    remainder(0, t, early_bank(number))
                    if 1 <= t <= DVE_LOW:
                        low(t - 1)
                    if t < CHUNKS:
                        norm_stats(CHUNKS + t)
                    if t == CHUNKS - 1:
                        norm_variance(1)
                    if CHUNKS <= t < 2 * CHUNKS:
                        if t == CHUNKS:
                            norm_root(1)
                        norm_apply(t)
                    if t == 2 * CHUNKS:
                        constants()
                elif job == "shift":
                    shift(t, t, early_bank(number))
                else:
                    for h in range(GH):
                        strip(0, t, h, unit, A_ROUND - EARLY_UNITS + unit)
                        unit += 1
                    if last_of_chunk(t) is not None:
                        chunk_max(last_of_chunk(t), unit)
                number += job != "strip"

            def read_jobs(i, jobs, s):
                for n, job in enumerate(jobs[s] if s >= 0 else []):
                    number = jobs_before(i, jobs, s) + n
                    if job[0] == "proj":
                        project(i + 1, job[1], number)
                    elif job[0] == "turn":
                        remainder(i + 1, job[1])
                    elif job[0] == "shift":
                        shift(job[2], (i * GROUPS + job[1]) * CHUNKS + job[2])
                    else:
                        normalise(i, job[1], number)

            def body(i, jobs, last):
                for s in range(BODY + 1):
                    units = [(g, k, h) for g, k in (strips_at(s) if s < BODY else [])
                             if not (last and g == GROUPS) for h in range(GH)]
                    for n, (g, k, h) in enumerate(units):
                        if n == DVE_AHEAD:
                            read_jobs(i, jobs, s - 1)
                        strip(g, k, h, unit_at(i, s) + n, UNITS[s] + n)
                        c = last_of_chunk(k)
                        if c is not None and h == GH - 1:
                            chunk_max(c, unit_at(i, s) + n + 1)
                    if len(units) <= DVE_AHEAD:
                        read_jobs(i, jobs, s - 1)
                read_jobs(i, jobs, BODY)

            rounds(dve, body)

            for p in range(2):
                dve.wait_ge(y_stored[p], NI * ENDS[BODY] // 2 * 16 + 1)
            for c in range(CT):
                nc.vector.tensor_reduce(xsum[:, c, :], xnT[:, c, :].rearrange("p (b t) -> p b t", b=B), AX_X,
                                        ALU.add).then_inc(glob_base, 1)
            dve.wait_ge(glob_base, 3 + CT)
            nc.vector.tensor_scalar(xsum[:], xsum[:], 1.0 / T, None, ALU.mult).then_inc(glob_base, 1)
            dve.wait_ge(glob_act, 3)
            nc.vector.tensor_scalar(base[:], gtanh[:], ar[:, 0:1], 0.7, ALU.mult, ALU.mult).then_inc(glob_base, 1)
            dve.wait_ge(glob_base, 5 + CT)
            nc.vector.tensor_scalar(base[:], base[:], 0.1, sign[:, 0:1], ALU.add, ALU.mult).then_inc(glob_base, 1)
            dve.wait_ge(glob_base, 6 + CT)

            for m in range(CYCLES * PAIRS):
                for blk in range(2):
                    n = 2 * m + blk
                    p = m % PAIRS
                    b = p * B // PAIRS
                    tok = slice((2 * p + blk) * QB, (2 * p + blk + 1) * QB)
                    dve.wait_ge(th_done, n + 1)
                    nc.vector.tensor_scalar(coup[:, blk, :], th[:, blk, :], swing[:, 0:1], base[:, b:b + 1],
                                            ALU.mult, ALU.add).then_inc(coup_done, 1)
                    dve.wait_ge(coup_done, n + 1)
                    for c in range(CT):
                        nc.vector.tensor_tensor(prod[:, blk, c, :], coup[:, blk, :], xnT[:, 1 - c, tok],
                                                ALU.mult).then_inc(prod_done, 1)
                    dve.wait_ge(prod_done, 2 * n + 2)
                    for c, op in ((0, ALU.add), (1, ALU.subtract)):
                        if m < (CYCLES - 1) * PAIRS:
                            nc.vector.tensor_tensor(xnT[:, c, tok], xnT[:, c, tok], prod[:, blk, c, :],
                                                    op).then_inc(upd_done, 1)
                        else:
                            nc.vector.scalar_tensor_tensor(xnT[:, c, tok], xnT[:, c, tok], bp_sb[:, c:c + 1],
                                                           prod[:, blk, c, :], ALU.add, op).then_inc(upd_done, 1)

            def add_coupling(t):
                k = t // TPC
                dve.wait_ge(turned_back, t + 1)
                dve.wait_ge(yx_loaded[k % INPUTS], (k // INPUTS + 1) * 48)
                nc.vector.tensor_tensor(x_res[:, k % INPUTS, t % TPC, :], ps_f[:, t % 2, 0:C],
                                        x_res[:, k % INPUTS, t % TPC, :], ALU.add).then_inc(half_sum, 1)

            add_coupling(0)
            for t in range(NT):
                k = t // TPC
                if t + 1 < NT:
                    add_coupling(t + 1)
                dve.wait_ge(sum_ready, t + 1)
                dve.wait_ge(half_sum, t + 1)
                if t % TPC == 0 and k >= 2:
                    dve.wait_ge(out_stored[k % 2], (k // 2) * 16)
                nc.vector.tensor_tensor(res[:, k % 2, t % TPC, :], ps_y[:, t % 2, 0:C],
                                        x_res[:, k % INPUTS, t % TPC, :], ALU.add).then_inc(res_ready, 1)

        @block.tensor
        def _(pe):
            def turn_x(k):
                pe.wait_ge(xn_ready, TPC * (k + 1))
                for c in range(CT):
                    n = k * CT + c
                    if n >= 2:
                        pe.wait_ge(xt_copied, n - 1)
                    for t in range(TPC):
                        last = nc.tensor.transpose(ps_x[:, n % 2, t * P:(t + 1) * P],
                                                   x_in[:, k * TPC + t, c * P:(c + 1) * P], ident[:])
                    last.then_inc(xt_ready, 1)

            pe.wait_ge(ident_loaded, 16)
            for k in range(CHUNKS):
                turn_x(k)

            def bank_free(r, i, job):
                if job[0] == "proj":
                    pe.wait_ge(v_ready, r * TILES + job[1] + 1)
                elif job[0] == "turn":
                    pe.wait_ge(rest_ready, r * TILES + job[1] + 1)
                elif job[0] == "shift":
                    pe.wait_ge(mrest_ready, (i * GROUPS + job[1]) * CHUNKS + job[2] + 1)
                else:
                    pe.wait_ge(y_ready, i * ENDS[BODY] + job[1] + 2)

            def project(r, t, bank=ps_j):
                if t == 0:
                    pe.wait_ge(w_loaded, (r + 1) * 32)
                cc = t // TPC
                if t % TPC == 0:
                    pe.wait_ge(win_loaded[cc % 2], (r * 2 + cc // 2 + 1) * 16)
                at = slice(t % TPC * P, (t % TPC + 1) * P)
                for c in range(CT):
                    last = nc.tensor.matmul(bank[:, 0:QKV], xwin[:, cc % 2, c, at], wcur[:, c, :],
                                            start=(c == 0), stop=(c == CT - 1))
                last.then_inc(job_ready, 1)

            def turn(r, t, bank=ps_j):
                pe.wait_ge(rot_done, r * TILES + t + 1)
                for side in range(2):
                    last = nc.tensor.transpose(bank[:, side * P:(side + 1) * P],
                                               qk_rot[:, t % 2, side * P:(side + 1) * P], ident[:])
                last.then_inc(job_ready, 1)

            def turn_max(n, c, bank=ps_j):
                pe.wait_ge(neg_ready, n + 1)
                nc.tensor.transpose(bank[0:GH * TPC, 0:P], neg_max[:, c % 2].rearrange("p h t -> p (h t)"),
                                    ident[:]).then_inc(job_ready, 1)

            def turn_out(i, n):
                pe.wait_ge(o_copied, i * ENDS[BODY] + n + 1)
                for t in range(TPC):
                    last = nc.tensor.transpose(ps_j[:, t * P:(t + 1) * P], o_sb[:, n % 2, t * P:(t + 1) * P],
                                               ident[:])
                last.then_inc(job_ready, 1)

            def strip(g, k, h, unit, place):
                t, kb, w = STRIPS[k]
                buf = g % GROUPS
                if not (isinstance(unit, int) and unit < RING):
                    pe.wait_ge(max_used, unit + 1 - ring_distance(place))
                nc.tensor.matmul(ps_m[:, place % RING, 0:w], qst[buf][0:ROWS, t // TPC, h, t % TPC * P:(t % TPC + 1) * P],
                                 kst[buf][0:ROWS, h, kb * QB:kb * QB + w], start=True, stop=True
                                 ).then_inc(max_ready, 1)

            def scores(i, s, h):
                g, n = divmod(s, NS)
                c, kt, lo = STEPS[n]
                if h == 0 and kt == 0:
                    pe.wait_ge(shift_loaded[c], (i * GROUPS + g + 1) * SHIFT_DMAS * 16)
                n = GH * s + h
                if not (isinstance(i, int) and i * A_ROUND + n < RING):
                    pe.wait_ge(exp_done, i * A_ROUND + n + 1 - ring_distance(n))
                nc.tensor.matmul(ps_s[:, n % RING, lo:], kst[g][0:KROWS, h, kt * P:(kt + 1) * P],
                                 qst[g][0:KROWS, c, h, lo:], start=True, stop=True
                                 ).then_inc(scores_ready, 1)

            def values(i, s):
                g, n = divmod(s, NS)
                c, kt, lo = STEPS[n]
                if diagonal(s):
                    pe.wait_ge(mask_done, i * DIAG[BODY] + DIAG[s] + 1)
                else:
                    pe.wait_ge(exp_done, i * A_ROUND + GH * (s + 1))
                if n == 0:
                    pe.wait_ge(v_loaded[g], (i + 1) * 16)
                if kt == 0 and s > 0:
                    pe.wait_ge(o_copied, i * ENDS[BODY] + ENDS[s])
                for h in range(GH):
                    last = nc.tensor.matmul(ps_o[2 * HS * h:2 * HS * h + VW, lo:], vcur[g][:, kt, h, :],
                                            probs[:, s % 2, h, lo:], start=(kt == 0),
                                            stop=(kt == TPC * (c + 1) - 1))
                last.then_inc(pv_done, 1)

            pe.wait_ge(pool_ones, 3)
            pe.wait_ge(zeros_set, 1)
            earlier = []
            unit = 0
            for job, t in EARLY:
                if job == "strip":
                    if t == 0 or last_of_chunk(t - 1) is not None:
                        pe.wait_ge(first_stack[STRIPS[t][0] // TPC], FIRST_STACK_DMAS * 16)
                    for h in range(GH):
                        strip(0, t, h, unit, A_ROUND - EARLY_UNITS + unit)
                        unit += 1
                    continue
                if len(earlier) >= 2:
                    bank_free(0, 0, earlier[-2])
                bank = early_bank(len(earlier))
                if job == "proj":
                    project(0, t, bank)
                elif job == "turn":
                    turn(0, t, bank)
                    if TPC < t <= 2 * TPC:
                        turn_x(t - 1)
                else:
                    turn_max(t, t, bank)
                earlier.append((job, 0, t) if job == "shift" else (job, t))
            for job in earlier[-2:]:
                bank_free(0, 0, job)
            pe.wait_ge(first_stack[CHUNKS - 1], FIRST_STACK_DMAS * 16)
            pe.wait_ge(xt_copied, CT * NT // TPC)
            for h in range(GH):
                scores(0, 0, h)
            early = len([k for _, k in EARLY_STRIPS if last_of_chunk(k) is not None])

            def small_jobs(i, jobs, before):
                for job in jobs:
                    if before:
                        bank_free(i + 1, i, before)
                    else:
                        pe.wait_ge(v_ready, (i + 1) * TILES)
                        pe.wait_ge(rest_ready, (i + 1) * TILES)
                        pe.wait_ge(mrest_ready, i * GROUPS * CHUNKS + early)
                        pe.wait_ge(y_ready, i * ENDS[BODY] + 1)
                    if job[0] == "proj":
                        project(i + 1, job[1])
                    elif job[0] == "turn":
                        turn(i + 1, job[1])
                    elif job[0] == "shift":
                        turn_max((i * GROUPS + job[1]) * CHUNKS + job[2], job[2])
                    else:
                        turn_out(i, job[1])
                    before = job
                return before

            def body(i, jobs, last):
                before = None
                for s in range(BODY + 1):
                    strips = [(g, k) for g, k in (strips_at(s) if s < BODY else []) if not (last and g == GROUPS)]
                    units = [(g, k, h) for g, k in strips for h in range(GH)]
                    for g, k in strips:
                        if k == 0:
                            pe.wait_ge(stack_loaded[g % GROUPS], (i + 1) * STACK_DMAS * 16)
                    number = 0
                    for place, few in enumerate(spread(units)):
                        for g, k, h in few:
                            strip(g, k, h, unit_at(i, s) + number, UNITS[s] + number)
                            number += 1
                        if place == VALUES_AT:
                            if s < BODY:
                                values(i, s)
                        elif place <= GH:
                            h = place - (place > VALUES_AT)
                            if s + 1 < BODY:
                                scores(i, s + 1, h)
                            elif s + 1 == BODY and not last:
                                scores(i + 1, 0, h)
                    before = small_jobs(i, jobs[s], before)

            rounds(pe, body)

            def layer_1(n, blk):
                p = n % PAIRS
                tok = slice((2 * p + blk) * QB, (2 * p + blk + 1) * QB)
                if n >= PAIRS:
                    pe.wait_ge(upd_done, 2 * (2 * (n - PAIRS) + blk + 1))
                for m in range(CT):
                    u = 4 * n + CT * blk + m
                    if u >= 2:
                        pe.wait_ge(g1_done, u - 1)
                    for c in range(CT):
                        last = nc.tensor.matmul(ps_1[:, m, :], w1[:, c, m * P:(m + 1) * P], xnT[:, c, tok],
                                                start=(c == 0), stop=(c == CT - 1))
                    last.then_inc(l1_done, 1)

            def layer_2(n, blk):
                pe.wait_ge(g1_done, 4 * n + CT * (blk + 1))
                if n >= 1:
                    pe.wait_ge(g2_done, 2 * (n - 1) + blk + 1)
                for c in range(CT):
                    last = nc.tensor.matmul(ps_2[:, blk, :], w2[:, c, :], h1[:, n % 2, blk, c, :],
                                            start=(c == 0), stop=(c == CT - 1))
                last.then_inc(l2_done, 1)

            def layer_3(n):
                pe.wait_ge(g2_done, 2 * n + 2)
                if n >= 1:
                    pe.wait_ge(g3_done, n)
                for blk in range(2):
                    last = nc.tensor.matmul(ps_3[H3 * blk:H3 * (blk + 1), :], w3[:], h2[:, n % 2, blk, :],
                                            start=True, stop=True)
                last.then_inc(l3_done, 1)

            def layer_4(n):
                pe.wait_ge(g3_done, n + 1)
                for blk in range(2):
                    if n >= 1:
                        pe.wait_ge(th_done, 2 * (n - 1) + blk + 1)
                    nc.tensor.matmul(ps_4[:, blk, :], w4_wide[:, blk, :], h3[:], start=True,
                                     stop=True).then_inc(l4_done, 1)

            def global_net(stage):
                if stage == 0:
                    pe.wait_ge(glob_base, 4 + CT)
                    for c in range(CT):
                        last = nc.tensor.matmul(ps_g[:, 0:B], gw1[:, c, :], xsum[:, c, :], start=(c == 0),
                                                stop=(c == CT - 1))
                else:
                    pe.wait_ge(glob_act, stage)
                    if stage == 1:
                        last = nc.tensor.matmul(ps_g[0:H3, 0:B], gw2[:], gh1[:], start=True, stop=True)
                    else:
                        last = nc.tensor.matmul(ps_g[:, 0:B], gw3_wide[:], gh2[:], start=True, stop=True)
                last.then_inc(glob_mm, 1)

            pe.wait_ge(exp_done, NI * A_ROUND)
            pe.wait_ge(y_ready, NI * ENDS[BODY] + 1)
            pe.wait_ge(prep, PREP)
            for n in range(CYCLES * PAIRS + 2):
                if n < CYCLES * PAIRS:
                    layer_1(n, 0)
                if n >= 2:
                    layer_3(n - 2)
                if n < CYCLES * PAIRS:
                    layer_1(n, 1)
                if n >= 2:
                    layer_4(n - 2)
                if n < 3:
                    global_net(n)
                if 1 <= n <= CYCLES * PAIRS:
                    for blk in range(2):
                        layer_2(n - 1, blk)

            def turn_y(t):
                k = t // TPC
                if t % TPC == 0:
                    pe.wait_ge(yx_loaded[k % INPUTS], (k // INPUTS + 1) * 48)
                if t >= RING:
                    pe.wait_ge(yt_copied, t - RING + 1)
                for c in range(CT):
                    last = nc.tensor.transpose(ps_t[:, t % RING, c * P:(c + 1) * P], y_in[:, k % INPUTS, t % TPC, c, :],
                                               ident[:])
                last.then_inc(yt_ready, 1)

            def turn_back(t):
                if t % TPC == 0:
                    pe.wait_ge(upd_done, 2 * (2 * (CYCLES - 1) * PAIRS + t // TPC + 1))
                if t >= 2:
                    pe.wait_ge(half_sum, t - 1)
                for c in range(CT):
                    last = nc.tensor.transpose(ps_f[:, t % 2, c * P:(c + 1) * P], xnT[:, c, t * P:(t + 1) * P],
                                               ident[:])
                last.then_inc(turned_back, 1)

            pe.wait_ge(g2_done, 2 * CYCLES * PAIRS)
            pe.wait_ge(g3_done, CYCLES * PAIRS)
            pe.wait_ge(th_done, 2 * CYCLES * PAIRS)
            for t in range(RING - 1):
                turn_y(t)
            turn_back(0)
            for t in range(NT):
                if t + RING - 1 < NT:
                    turn_y(t + RING - 1)
                if t + 1 < NT:
                    turn_back(t + 1)
                pe.wait_ge(yt_copied, t + 1)
                if t >= 2:
                    pe.wait_ge(res_ready, t - 1)
                for c in range(CT):
                    last = nc.tensor.matmul(ps_y[:, t % 2, 0:C], yT[:, t % RING, c, :], wp_sb[:, c, :],
                                            start=(c == 0), stop=(c == CT - 1))
                last.then_inc(sum_ready, 1)


_FFN = ["cn_w1", "cn_b1", "cn_w2", "cn_b2", "cn_w3", "cn_b3", "cn_w4", "cn_b4", "gc_w1", "gc_b1", "gc_w2", "gc_b2",
        "gc_w3", "gc_b3", "adaptive_range"]


def rope_tables():
    half = HS // 2
    inv_freq = (np.float32(1.0) / np.float32(10000.0) ** (np.arange(half, dtype=np.float32) * np.float32(2.0)
                                                          / np.float32(HS))).astype(np.float32)
    ang = np.arange(T, dtype=np.float32)[:, None] * inv_freq[None, :]
    cos = np.repeat(np.cos(ang), 2, axis=1)
    sin = np.stack([-np.sin(ang), np.sin(ang)], axis=-1).reshape(T, HS)
    return [np.ascontiguousarray(a.astype(np.float32).reshape(TILES, P, HS).transpose(1, 0, 2)) for a in (cos, sin)]


def by_partition(v):
    return np.ascontiguousarray(v.reshape(CT, P).T)


def kernel(**inputs):
    import concourse.bacc as bacc
    from concourse.bass_utils import run_bass_kernel_spmd

    a = {k: np.ascontiguousarray(v) for k, v in inputs.items()}
    by_head = np.arange(P)
    by_dim = by_head.reshape(GROUPS, GH, HS).transpose(0, 2, 1).reshape(P)
    halves = [[P * (i % CT) + order for order in (by_dim, by_dim, by_head)] for i in range(NI)]
    wqkv = np.stack([np.concatenate([a[f"L0_attn_W{n}"][:, h] for n, h in zip("qkv", half)], axis=1)
                     for half in halves])
    bqkv = np.stack([np.concatenate([a[f"L0_attn_b{n}"][h] for n, h in zip("qkv", half)]) for half in halves])
    cos, sin = rope_tables()
    arrays = {
        "x": a["L0_attn_x"], "wqkv": wqkv, "bqkv": np.ascontiguousarray(np.broadcast_to(bqkv[:, None], (NI, P, QKV))),
        "wp": a["L0_attn_Wp"], "bp": by_partition(a["L0_attn_bp"]), "cos": cos, "sin": sin, "ident": np.eye(P, dtype=np.float32),
    }
    for n in _FFN:
        arrays[n] = a[f"L0_ffn_{n}"]
    arrays["cn_b1"] = by_partition(arrays["cn_b1"])
    nc = bacc.Bacc("TRN2", target_bir_lowering=False, num_devices=1)
    ap = {n: nc.dram_tensor(f"{n}_dram", v.shape, F32, kind="ExternalInput").ap() for n, v in arrays.items()}
    out = nc.dram_tensor("out_dram", (B, T, C), F32, kind="ExternalOutput").ap()
    y_dram = nc.dram_tensor("y_scratch", (NI, T, P), F32, kind="Internal").ap()
    build(nc, ap["x"], ap["wqkv"], ap["bqkv"], ap["wp"], ap["bp"], ap["cos"], ap["sin"], ap["ident"],
          {n: ap[n] for n in _FFN}, out, y_dram)
    r = run_bass_kernel_spmd(nc, [{f"{n}_dram": v for n, v in arrays.items()}], core_ids=[0])
    return r.results[0]["out_dram"]
```
